# Optimizing a Trainium2 kernel written in Bass

```python
import numpy as np
import jax
import jax.numpy as jnp

def _softmax(x, axis=-1):
    return jax.nn.softmax(x, axis=axis)

def _gelu(x):
    return jax.nn.gelu(x, approximate=True)

def _silu(x):
    return jax.nn.silu(x)

def _sigmoid(x):
    return jax.nn.sigmoid(x)

def _layernorm(x, axis=-1, eps=1e-05):
    m = jnp.mean(x, axis=axis, keepdims=True)
    v = jnp.var(x, axis=axis, keepdims=True)
    return (x - m) / jnp.sqrt(v + eps)

def _scatter_add(tgt, idx, src, axis=0):
    return tgt.at[idx].add(src)

def _segment_sum(src, seg, n):
    return jax.ops.segment_sum(src, seg, n)
kernel_name = 'mk_vit_tower_d1_tok_img1024_r4_2e0b2f'

def setup_inputs(seed: int=0):
    np.random.seed(seed)
    _w = jnp.asarray

    def _rec_inputs():
        import jax
        import jax.numpy as jnp
        _rk = jax.random.key(seed)
        x = -0.00016672 + 0.999947 * jax.random.normal(jax.random.fold_in(_rk, 1), (16, 3, 96, 96), jnp.float32)
        return x
    x = _rec_inputs()

    def _L0_tok_setup():
        import jax, jax.numpy as jnp
        import numpy as np
        B, C, H, Wd = (64, 3, 96, 96)
        PH, PW, D = (16, 16, 256)
        PATCH_DIM = C * PH * PW
        N_TOK = H // PH * (Wd // PW)
        key = jax.random.key(seed)
        k1, k2, k3, k4, k5 = jax.random.split(key, 5)
        x = jax.random.normal(k1, (B, C, H, Wd), dtype=jnp.float32)
        W = jax.random.normal(k2, (D, PATCH_DIM), dtype=jnp.float32) * PATCH_DIM ** (-0.5)
        b = jax.random.normal(k3, (D,), dtype=jnp.float32) * 0.02
        cls_token = jax.random.normal(k4, (1, 1, D), dtype=jnp.float32)
        pos_embedding = jax.random.normal(k5, (1, N_TOK + 1, D), dtype=jnp.float32) * 0.02
        return {'x': x, 'W': W, 'b': b, 'cls_token': cls_token, 'pos_embedding': pos_embedding}
    _L0_tok_all = _L0_tok_setup()
    _L0_tok_in = {k: v for k, v in _L0_tok_all.items() if k in ('W', 'b', 'cls_token', 'pos_embedding')}
    del _L0_tok_all

    def _L0_attn_setup():
        import jax, jax.numpy as jnp
        import numpy as np
        B, S, DIN, DIM = (1, 1024, 256, 256)
        NH, NKV = (16, 4)
        HD = DIM // NH
        GS = NH // NKV
        key = jax.random.key(seed)
        ks = jax.random.split(key, 5)

        def w(k, shape, fan_in):
            return jax.random.normal(k, shape, jnp.float32) * fan_in ** (-0.5)
        return {'x': jax.random.normal(ks[0], (B, S, DIN), jnp.float32), 'wq': w(ks[1], (DIM, DIN), DIN), 'wk': w(ks[2], (NKV * HD, DIN), DIN), 'wv': w(ks[3], (NKV * HD, DIN), DIN), 'wo': w(ks[4], (DIM, DIM), DIM)}
    _L0_attn_all = _L0_attn_setup()
    _L0_attn_in = {k: v for k, v in _L0_attn_all.items() if k in ('wq', 'wk', 'wv', 'wo')}
    del _L0_attn_all

    def _L0_ffn_setup():
        import jax, jax.numpy as jnp
        import numpy as np
        NUM_EXPERTS = 8
        NUM_SELECTED = 2
        EXPERT_CAPACITY = 128
        NUM_GROUPS = 8

        def _routing(xg, w_router):
            G, T, H = xg.shape
            logits = jnp.einsum('gth,he->gte', xg, w_router)
            probs = jax.nn.softmax(logits, axis=-1)
            _gate, idx = jax.lax.top_k(probs, NUM_SELECTED)
            idx_kt = jnp.swapaxes(idx, 1, 2).reshape(G, -1)
            expert_mask = jax.nn.one_hot(idx_kt, NUM_EXPERTS, dtype=jnp.int32)
            priority = jnp.cumsum(expert_mask, axis=1) * expert_mask - 1
            priority = priority.reshape(G, NUM_SELECTED, T, NUM_EXPERTS)
            priority = jnp.swapaxes(priority, 1, 2).max(axis=2)
            dispatch = jax.nn.one_hot(priority, EXPERT_CAPACITY, dtype=xg.dtype)
            combine = probs[..., None] * dispatch
            return (dispatch, combine)
        key = jax.random.key(seed)
        k1, k2, k3, k4 = jax.random.split(key, 4)
        B, S, H, F = (8, 512, 256, 1024)
        return {'x': jax.random.normal(k1, (B, S, H), jnp.float32), 'w_router': jax.random.normal(k2, (H, NUM_EXPERTS), jnp.float32) * 0.02, 'wi': jax.random.normal(k3, (NUM_EXPERTS, H, F), jnp.float32) * 0.02, 'wo': jax.random.normal(k4, (NUM_EXPERTS, F, H), jnp.float32) * 0.02}
    _L0_ffn_all = _L0_ffn_setup()
    _L0_ffn_in = {k: v for k, v in _L0_ffn_all.items() if k in ('w_router', 'wi', 'wo')}
    del _L0_ffn_all
    return {'x': x, 'L0_tok_W': _L0_tok_in['W'], 'L0_tok_b': _L0_tok_in['b'], 'L0_tok_cls_token': _L0_tok_in['cls_token'], 'L0_tok_pos_embedding': _L0_tok_in['pos_embedding'], 'L0_attn_wq': _L0_attn_in['wq'], 'L0_attn_wk': _L0_attn_in['wk'], 'L0_attn_wv': _L0_attn_in['wv'], 'L0_attn_wo': _L0_attn_in['wo'], 'L0_ffn_w_router': _L0_ffn_in['w_router'], 'L0_ffn_wi': _L0_ffn_in['wi'], 'L0_ffn_wo': _L0_ffn_in['wo']}

def reference(x, L0_tok_W, L0_tok_b, L0_tok_cls_token, L0_tok_pos_embedding, L0_attn_wq, L0_attn_wk, L0_attn_wv, L0_attn_wo, L0_ffn_w_router, L0_ffn_wi, L0_ffn_wo):
    import jax
    import jax.numpy as jnp

    def _L0_tok_ref(x, W, b, cls_token, pos_embedding):
        import jax, jax.numpy as jnp
        import numpy as np
        B, C, H, Wd = (64, 3, 96, 96)
        PH, PW, D = (16, 16, 256)
        PATCH_DIM = C * PH * PW
        N_TOK = H // PH * (Wd // PW)
        Bc = x.shape[0]
        nh, nw = (H // PH, Wd // PW)
        patches = x.reshape(Bc, C, nh, PH, nw, PW)
        patches = patches.transpose(0, 2, 4, 1, 3, 5).reshape(Bc, nh * nw, PATCH_DIM)
        tokens = jnp.einsum('bnp,dp->bnd', patches, W) + b
        cls = jnp.broadcast_to(cls_token, (Bc, 1, D))
        tokens = jnp.concatenate([cls, tokens], axis=1)
        return tokens + pos_embedding

    def _L0_attn_ref(x, wq, wk, wv, wo):
        import jax, jax.numpy as jnp
        import numpy as np
        B, S, DIN, DIM = (1, 1024, 256, 256)
        NH, NKV = (16, 4)
        HD = DIM // NH
        GS = NH // NKV
        b, s, _ = x.shape
        q = (x @ wq.T).reshape(b, s, NKV, GS, HD)
        k = (x @ wk.T).reshape(b, s, NKV, HD)
        v = (x @ wv.T).reshape(b, s, NKV, HD)
        scale = jnp.asarray(HD ** 0.5, x.dtype)
        att = jnp.einsum('bsgmd,btgd->bgmst', q, k) / scale
        causal = jnp.triu(jnp.ones((s, s), bool), 1)
        att = jnp.where(causal, -jnp.inf, att)
        att = jax.nn.softmax(att, axis=-1)
        ctx = jnp.einsum('bgmst,btgd->bsgmd', att, v).reshape(b, s, DIM)
        return ctx @ wo.T

    def _L0_ffn_ref(x, w_router, wi, wo):
        import jax, jax.numpy as jnp
        import numpy as np
        NUM_EXPERTS = 8
        NUM_SELECTED = 2
        EXPERT_CAPACITY = 128
        NUM_GROUPS = 8

        def _routing(xg, w_router):
            G, T, H = xg.shape
            logits = jnp.einsum('gth,he->gte', xg, w_router)
            probs = jax.nn.softmax(logits, axis=-1)
            _gate, idx = jax.lax.top_k(probs, NUM_SELECTED)
            idx_kt = jnp.swapaxes(idx, 1, 2).reshape(G, -1)
            expert_mask = jax.nn.one_hot(idx_kt, NUM_EXPERTS, dtype=jnp.int32)
            priority = jnp.cumsum(expert_mask, axis=1) * expert_mask - 1
            priority = priority.reshape(G, NUM_SELECTED, T, NUM_EXPERTS)
            priority = jnp.swapaxes(priority, 1, 2).max(axis=2)
            dispatch = jax.nn.one_hot(priority, EXPERT_CAPACITY, dtype=xg.dtype)
            combine = probs[..., None] * dispatch
            return (dispatch, combine)
        B, S, H = x.shape
        T = B * S // NUM_GROUPS
        xg = x.reshape(NUM_GROUPS, T, H)
        dispatch, combine = _routing(xg, w_router)
        expert_in = jnp.einsum('gth,gtec->gech', xg, dispatch)
        h = jax.nn.gelu(jnp.einsum('gech,ehf->gecf', expert_in, wi))
        expert_out = jnp.einsum('gecf,efh->gech', h, wo)
        out = jnp.einsum('gech,gtec->gth', expert_out, combine)
        return out.reshape(B, S, H)
    h = _L0_tok_ref(x, L0_tok_W, L0_tok_b, L0_tok_cls_token, L0_tok_pos_embedding)
    h = h + _L0_attn_ref(_layernorm(h, axis=-1), L0_attn_wq, L0_attn_wk, L0_attn_wv, L0_attn_wo)
    h = h + _L0_ffn_ref(_layernorm(h, axis=-1), L0_ffn_w_router, L0_ffn_wi, L0_ffn_wo)
    return h

_drawn_inputs = setup_inputs


def setup_inputs(seed=0):
    import zlib

    import numpy as np

    out = dict(_drawn_inputs(seed))
    spreads = {}
    factors = {'L0_tok_pos_embedding': 2.708, 'L0_ffn_w_router': 2.749}
    for name, (base, spread) in spreads.items():
        noise = np.random.default_rng([zlib.crc32(name.encode()), seed]).standard_normal(out[name].shape)
        drawn = base * np.exp(spread * noise) if base else spread * noise
        out[name] = jnp.asarray(drawn.astype(out[name].dtype))
    for name, factor in factors.items():
        out[name] = (out[name] * factor).astype(out[name].dtype)
    return out
```

```python
from contextlib import ExitStack

import numpy as np

import concourse.bass as bass
from concourse import mybir

F32 = mybir.dt.float32
BF16 = mybir.dt.bfloat16
I32 = mybir.dt.int32
ALU = mybir.AluOpType
ACT = mybir.ActivationFunctionType
AX = mybir.AxisListType

P = 128
B, C, IMG, PATCH, D = 16, 3, 96, 16, 256
GRID = IMG // PATCH
S = GRID * GRID + 1
N = B * S
NC = -(-N // P)
NP = NC * P
LAST = N - (NC - 1) * P
KP = C * PATCH * PATCH // P
KD = D // P
NKV, GS, HD = 4, 4, 16
GT = NKV * S
MS = 2 * S
G2 = 2 * (HD + 1)
IG = 2
NG = B // IG
HALF = N // 2
E, F, TOPK = 8, 1024, 2
FC = F // P
TILES = (N * TOPK + E * (P - 1)) // P
EPS = 1e-5
NEWTON = 4
NEG = -1e30

C_IDENT = 0
C_AMASK = C_IDENT + P
C_GMASK = C_AMASK + GT
C_VMASK = C_GMASK + NKV
C_UPPER = C_VMASK + 2
C_VALID = C_UPPER + P
C_REVERSED = C_VALID + NC
C_TILE = C_REVERSED + E
C_END = C_TILE + TILES


def constants():
    c = np.zeros((P, C_END), np.float32)
    p = np.arange(P)
    c[:, C_IDENT:C_IDENT + P] = np.eye(P)
    c[:, C_AMASK:C_AMASK + GT] = np.where(np.arange(GT)[None] % S > p[:, None] % S, NEG, 0.0)
    c[:, C_GMASK:C_GMASK + NKV] = (p[:, None] % (NKV * HD)) // HD == np.arange(NKV)[None]
    c[:, C_VMASK:C_VMASK + 2] = p[:, None] // S == np.arange(2)[None]
    c[:, C_UPPER:C_UPPER + P] = p[:, None] < p[None]
    c[:, C_VALID:C_VALID + NC] = np.arange(NC)[None] * P + p[:, None] < N
    c[:, C_REVERSED:C_REVERSED + E] = E - np.arange(E)[None]
    c[:, C_TILE:C_TILE + TILES] = np.arange(TILES)[None]
    return c


def position_rows():
    n = np.arange(NP)
    rows = np.zeros((S + 2, NP), np.float32)
    for s in range(S):
        rows[s] = (n % S == s) & (n < N)
    rows[S] = (n % S != 0) & (n < N)
    rows[S + 1] = (n % S == 0) & (n < N)
    return rows


def vit_block(nc, patches, w_tok, bias, cls, pos, wq, wk, wv, wo, w_router, wi, w2, consts, pos_rows, out):
    ctx = ExitStack()
    with ctx:
        def sb(name, shape, dt=F32):
            return ctx.enter_context(nc.sbuf_tensor(name, shape, dt))

        def sem(name):
            return ctx.enter_context(nc.semaphore(name))

        rows_in = nc.dram_tensor("rows_in", [TILES * P, D], F32, kind="Internal").ap()
        rows_out = nc.dram_tensor("rows_out", [TILES * P, D], F32, kind="Internal").ap()

        wi_sb = sb("wi_sb", [P, E * KD * F])
        w2_sb = sb("w2_sb", [P, E * FC * D])
        early = sb("early", [P, KP * NP])
        patches_sb = early[:, :].rearrange("p (k n) -> p k n", n=NP)
        hid = early[:, 0:2 * F].rearrange("p (i k n) -> p i k n", i=2, n=P)
        hidT = early[:, 2 * F:3 * F].rearrange("p (k n) -> p k n", n=P)
        y_sb = early[:, 3 * F:3 * F + 2 * D].rearrange("p (i d) -> p i d", d=D)
        ctxT = early[:, 0:2 * NP].rearrange("p (m n) -> p m n", m=2)
        at = 2 * NP
        prob = early[0:MS, at:at + 4 * IG * GT].rearrange("p (i m g t) -> p i m g t", i=2, m=2, t=S)
        at += 4 * IG * GT
        probT = early[0:MS, at:at + 4 * IG * MS].rearrange("p (b n) -> p b n", b=IG)
        twice = early[:, 2 * NP:2 * NP + KD * B * MS].rearrange("p (k b i s) -> p k b i s", k=KD, b=B, i=2)
        w_tok_sb = sb("w_tok_sb", [P, KP, D])
        x_sb = w_tok_sb[:, 0:2, :]
        x_T = w_tok_sb[:, 2:4, :]
        pos_rows_sb = sb("pos_rows_sb", [S + 2, NP])
        pos_sb = sb("pos_sb", [S + 2, D])
        cst = sb("cst", [P, C_END])
        wq_sb = sb("wq_sb", [P, KD, 2, P])
        wk_sb = sb("wk_sb", [P, KD, 2, NKV * HD])
        wv_sb = sb("wv_sb", [P, KD, NKV * HD])
        wo_sb = sb("wo_sb", [P, 2, D])
        wr_sb = sb("wr_sb", [P, KD, E])
        amask = sb("amask", [P, GT], BF16)
        ident_bf = sb("ident_bf", [P, P], BF16)
        upper_bf = sb("upper_bf", [P, P], BF16)
        ones_bf = sb("ones_bf", [P, P], BF16)
        h = sb("h", [P, NC, D])
        xn = sb("xn", [P, NC, D])
        xnT = sb("xnT", [P, KD, NP])
        stats = sb("stats", [P, NC, 6])
        mv = sb("mv", [P, NC, 2])
        var = sb("var", [P, NC])
        guess = sb("guess", [P, NC], I32)
        newton = sb("newton", [P, NC])
        rstd = sb("rstd", [P, NC])
        middle = sb("middle", [P, B * (MS + GT)])
        qT = middle[:, 0:B * MS].rearrange("p (b m s) -> p b m s", m=2, s=S)
        kbd = middle[:, B * MS:B * (MS + GT)].rearrange("p (b g t) -> p b g t", g=NKV, t=S)
        picked = middle[:, 0:TOPK * NC * D].rearrange("p (c d) -> p c d", d=D)
        vbd = sb("vbd", [MS, B * 2, 2, HD + 1])
        q_st = sb("q_st", [P, 2, IG * MS])
        k_st = sb("k_st", [P, 2, IG * GT])
        top = sb("top", [MS, 2, 2, IG * NKV])
        rsum = sb("rsum", [MS, 4 * NKV])
        ctxn = sb("ctxn", [MS, IG, 2 * NKV * HD])
        zeros = sb("zeros", [P, D])
        lg = sb("lg", [P, NC, E])
        lg2 = sb("lg2", [P, NC, E])
        mx = sb("mx", [P, 2, NC])
        eq = sb("eq", [P, NC, E])
        rv = sb("rv", [P, NC])
        mask = sb("mask", [P, 2, NC, E])
        ex = sb("ex", [P, NC, E])
        den = sb("den", [P, NC])
        gate = sb("gate", [P, 2, NC])
        both = sb("both", [P, NC, E], BF16)
        count = sb("count", [P, NC + 1, E])
        rank = sb("rank", [P, NC, E])
        over = sb("over", [P, E, NC])
        used = sb("used", [P, E])
        ones8 = sb("ones8", [P, E])
        end = sb("end", [P, E])
        start = sb("start", [P, E])
        slot_e = sb("slot_e", [P, NC, E])
        slot_f = sb("slot_f", [P, 2, NC])
        slot = sb("slot", [P, 2, NC], I32)
        le = sb("le", [P, TILES, E])
        eid_f = sb("eid_f", [P, TILES])
        eid = sb("eid", [P, TILES], I32)

        ident = cst[:, C_IDENT:C_IDENT + P]

        ps = ctx.enter_context(nc.psum_tensor("ps", [P, 8, 512], F32))

        pos_in = sem("pos_in")
        patch_in = [sem(f"patch_in{i}") for i in range(KP // 2)]
        const_in = sem("const_in")
        attn_in = sem("attn_in")
        ffn_in = sem("ffn_in")
        cleared = sem("cleared")
        zero_rows = sem("zero_rows")
        const_ready = sem("const_ready")
        tok_done = sem("tok_done")
        h_ready = sem("h_ready")
        xn_ready = sem("xn_ready")
        xnT_done = sem("xnT_done")
        xnT_ready = sem("xnT_ready")
        twice_ready = sem("twice_ready")
        q_done = sem("q_done")
        q_ready = sem("q_ready")
        k_done = sem("k_done")
        k_ready = sem("k_ready")
        v_done = sem("v_done")
        v_ready = sem("v_ready")
        staged = sem("staged")
        s_done = sem("s_done")
        top_ready = sem("top_ready")
        shifted = sem("shifted")
        p_ready = sem("p_ready")
        pT_done = sem("pT_done")
        pT_even = sem("pT_even")
        pT_odd = sem("pT_odd")
        c_done = sem("c_done")
        rsum_ready = sem("rsum_ready")
        ctxn_ready = sem("ctxn_ready")
        cT_done = sem("cT_done")
        ctxT_ready = sem("ctxT_ready")
        wo_done = sem("wo_done")
        xn2_ready = sem("xn2_ready")
        xn2T_done = sem("xn2T_done")
        xn2T_ready = sem("xn2T_ready")
        logits_done = sem("logits_done")
        logit_shift = sem("logit_shift")
        ex_ready = sem("ex_ready")
        both_ready = sem("both_ready")
        count_done = sem("count_done")
        slots_ready = sem("slots_ready")
        eid_ready = sem("eid_ready")
        scattered = sem("scattered")
        x_in = [sem(f"x_in{i}") for i in range(2)]
        xT_done = sem("xT_done")
        xT_ready = sem("xT_ready")
        up_done = sem("up_done")
        hid_ready = sem("hid_ready")
        hT_done = sem("hT_done")
        hT_ready = sem("hT_ready")
        y_done = sem("y_done")
        y_ready = sem("y_ready")
        y_out = [sem(f"y_out{i}") for i in range(2)]
        picked_in = sem("picked_in")
        out_ready = sem("out_ready")
        out_sent = sem("out_sent")
        step = sem("step")

        block = ctx.enter_context(nc.Block())

        @block.sync
        def _(sp):
            sp.dma_start(pos_rows_sb[:, :], pos_rows).then_inc(pos_in, 16)
            sp.dma_start(pos_sb[0:S, :], pos[0, :, :]).then_inc(pos_in, 16)
            sp.dma_start(pos_sb[S:S + 1, :], bias.rearrange("(a d) -> a d", a=1)).then_inc(pos_in, 16)
            sp.dma_start(pos_sb[S + 1:S + 2, :], cls[0, :, :]).then_inc(pos_in, 16)
            for i in range(KP // 2):
                k = slice(2 * i, 2 * i + 2)
                sp.dma_start(w_tok_sb[:, k, :], w_tok[:, k, :]).then_inc(patch_in[i], 16)
                sp.dma_start(patches_sb[:, k, :], patches[:, k, :]).then_inc(patch_in[i], 16)
            sp.dma_start(cst[:, :], consts).then_inc(const_in, 16)
            sp.dma_start(wq_sb[:, :, :, :], wq).then_inc(attn_in, 16)
            for i in range(2):
                sp.dma_start(wk_sb[:, :, i, :], wk).then_inc(attn_in, 16)
            sp.dma_start(wv_sb[:, :, :], wv).then_inc(attn_in, 16)
            sp.dma_start(wo_sb[:, :, :], wo).then_inc(attn_in, 16)
            sp.dma_start(wr_sb[:, :, :], w_router.rearrange("(k p) e -> p k e", p=P)).then_inc(attn_in, 16)
            sp.wait_ge(cleared, 1)
            sp.dma_start(rows_in.rearrange("(t p) d -> p t d", p=P),
                         zeros[:, :].unsqueeze(1).to_broadcast([P, TILES, D])).then_inc(zero_rows, 16)
            for e in range(E):
                sp.dma_start(wi_sb[:, e * KD * F:(e + 1) * KD * F].rearrange("p (k f) -> p k f", f=F),
                             wi[e, :, :].rearrange("(k p) f -> p k f", p=P)).then_inc(ffn_in, 16)
                sp.dma_start(w2_sb[:, e * FC * D:(e + 1) * FC * D],
                             w2[e, :, :].rearrange("(p k) d -> p (k d)", p=P)).then_inc(ffn_in, 16)

            def load(t, i):
                sp.dma_start(x_sb[:, i, :], rows_in[bass.ds(t * P, P), :]).then_inc(x_in[i], 16)

            def store(t, i):
                sp.wait_ge(y_ready, t + 1)
                sp.dma_start(rows_out[bass.ds(t * P, P), :], y_sb[:, i, :]).then_inc(y_out[i], 16)

            sp.wait_ge(scattered, 16 * TOPK * NC)
            load(0, 0)
            load(1, 1)
            with sp.Fori(0, (TILES - 3) // 2) as k:
                for i in range(2):
                    sp.wait_ge(xT_done, 2 * k + i + 1)
                    load(2 * k + i + 2, i)
                    store(2 * k + i, i)
            sp.wait_ge(xT_done, TILES - 2)
            load(TILES - 1, 0)
            for t in range(TILES - 3, TILES):
                store(t, t % 2)
            for c in range(NC):
                n = P if c < NC - 1 else LAST
                sp.wait_ge(out_ready, c + 1)
                sp.dma_start(out[c * P:c * P + n, :], h[0:n, c, :]).then_inc(out_sent, 16)
            sp.wait_ge(out_sent, 16 * NC)

        @block.gpsimd
        def _(pool):
            pool.memset(zeros[:, :], 0.0).then_inc(cleared, 1)
            pool.wait_ge(tok_done, NC)
            pool.memset(ctxT[:, :, N:NP], 0.0).then_inc(cleared, 1)

            def stage(i, par):
                pool.tensor_copy(q_st[:, par, :], qT[:, :, :, :].rearrange("p b m s -> p (b m s)")
                                 [:, bass.ds(i * IG * MS, IG * MS)]).then_inc(staged, 1)
                pool.tensor_copy(k_st[:, par, :], kbd[:, :, :, :].rearrange("p b g t -> p (b g t)")
                                 [:, bass.ds(i * IG * GT, IG * GT)]).then_inc(staged, 1)

            pool.wait_ge(q_ready, 4)
            pool.wait_ge(k_ready, 2 * NKV)
            stage(0, 0)
            stage(1, 1)
            with pool.Fori(0, NG // 2 - 1) as k:
                for i in range(2):
                    pool.wait_ge(s_done, 2 * (2 * k + i + 1))
                    stage(2 * k + i + 2, i)

            pool.wait_ge(zero_rows, 16)
            pool.wait_ge(slots_ready, 1)
            pool.wait_ge(xn2_ready, NC)
            for j in range(TOPK):
                for c in range(NC):
                    n = P if c < NC - 1 else LAST
                    pool.indirect_dma_start(
                        out=rows_in, out_offset=bass.IndirectOffsetOnAxis(ap=slot[0:n, j, c:c + 1], axis=0),
                        in_=xn[0:n, c, :], in_offset=None).then_inc(scattered, 16)
            for i in range(2):
                pool.wait_ge(y_out[i], 16 * ((TILES + 1 - i) // 2))
            for c in range(NC):
                for j in range(TOPK):
                    n = P if c < NC - 1 else LAST
                    pool.indirect_dma_start(
                        out=picked[0:n, c * TOPK + j, :], out_offset=None, in_=rows_out,
                        in_offset=bass.IndirectOffsetOnAxis(ap=slot[0:n, j, c:c + 1], axis=0)
                    ).then_inc(picked_in, 16)

        @block.scalar
        def _(act):
            for c in range(NC):
                act.wait_ge(tok_done, c + 1)
                act.activation(h[:, c, :], ps[:, c, 0:D], ACT.Copy).then_inc(h_ready, 1)
            for c in range(NC):
                act.wait_ge(xnT_done, c + 1)
                act.activation(xnT[:, :, c * P:(c + 1) * P],
                               ps[:, 5 + c % 3, 0:D].rearrange("p (k n) -> p k n", k=KD),
                               ACT.Copy).then_inc(xnT_ready, 1)
            for m in range(2):
                for j in range(2):
                    act.wait_ge(q_done, 2 * m + j + 1)
                    act.activation(qT[:, 8 * j:8 * j + 8, m, :],
                                   ps[:, 2 * m + j, 0:HALF].rearrange("p (b s) -> p b s", s=S),
                                   ACT.Copy).then_inc(q_ready, 1)

            def exps(i, par):
                act.wait_ge(shifted, i + 1)
                act.activation(prob[:, par, :, :, :], prob[:, par, :, :, :], ACT.Exp,
                               scale=HD ** -0.5).then_inc(p_ready, 1)

            def probs_out(i):
                act.wait_ge(pT_done, 2 * i + 1)
                act.activation(probT[:, 0, :], ps[0:MS, 4, 0:4 * MS], ACT.Copy).then_inc(pT_even, 1)

            def context_out(i):
                act.wait_ge(cT_done, i + 1)
                act.activation(
                    ctxT[:, :, bass.ds(i * IG * S, IG * S)].rearrange("p m (b s) -> p b m s", s=S),
                    ps[:, 7, 0:IG * MS].rearrange("p (b m s) -> p b m s", b=IG, m=2),
                    ACT.Copy).then_inc(ctxT_ready, 1)

            exps(0, 0)
            exps(1, 1)
            with act.Fori(0, NG // 2 - 1) as k:
                for i in range(2):
                    probs_out(2 * k + i)
                    context_out(2 * k + i)
                    exps(2 * k + i + 2, i)
            for i in range(NG - 2, NG):
                probs_out(i)
                context_out(i)

            for c in range(NC):
                act.wait_ge(xn2T_done, c + 1)
                act.activation(xnT[:, :, c * P:(c + 1) * P],
                               ps[:, 5 + c % 2, 0:D].rearrange("p (k n) -> p k n", k=KD),
                               ACT.Copy).then_inc(xn2T_ready, 1)
            act.wait_ge(logit_shift, 1)
            act.activation(ex[:, :, :], ex[:, :, :], ACT.Exp).then_inc(ex_ready, 1)

            def hidden(t, i):
                for half in range(2):
                    act.wait_ge(up_done, 2 * t + half + 1)
                    if half == 0 and not (isinstance(t, int) and t < 2):
                        act.wait_ge(hT_done, 2 * (t - 1))
                    act.activation(
                        hid[:, i, :, half * 64:half * 64 + 64].rearrange("p k q -> p q k"),
                        ps[:, half, :].rearrange("p (q k) -> p q k", k=FC),
                        ACT.Gelu_apprx_tanh).then_inc(hid_ready, 1)

            hidden(0, 0)
            hidden(1, 1)
            with act.Fori(0, (TILES - 3) // 2) as k:
                for i in range(2):
                    hidden(2 * k + i + 2, i)
            hidden(TILES - 1, 0)

        @block.vector
        def _(dve):
            steps = [0]

            def chain(ins):
                steps[0] += 1
                ins.then_inc(step, 1)
                dve.wait_ge(step, steps[0])

            dve.memset(ones_bf[:, :], 1.0).then_inc(const_ready, 1)
            dve.memset(ones8[:, :], 1.0).then_inc(const_ready, 1)
            dve.wait_ge(const_in, 16)
            dve.tensor_copy(amask[:, :], cst[:, C_AMASK:C_AMASK + GT]).then_inc(const_ready, 1)
            dve.tensor_copy(ident_bf[:, :], ident).then_inc(const_ready, 1)
            dve.tensor_copy(upper_bf[:, :], cst[:, C_UPPER:C_UPPER + P]).then_inc(const_ready, 1)

            def normalise(ready):
                for c in range(NC):
                    chain(dve.bn_aggr(mv[:, c, :], stats[:, c, :]))
                chain(dve.tensor_scalar(var[:, :], mv[:, :, 1], EPS, None, ALU.add))
                chain(dve.tensor_scalar(guess[:, :], var[:, :].bitcast(I32), 1, None, ALU.logical_shift_right))
                chain(dve.tensor_scalar(rstd[:, :].bitcast(I32), guess[:, :], -1.0, float(0x5F3759DF),
                                        ALU.mult, ALU.add))
                for _ in range(NEWTON):
                    chain(dve.tensor_tensor(newton[:, :], var[:, :], rstd[:, :], ALU.mult))
                    chain(dve.scalar_tensor_tensor(newton[:, :], newton[:, :], -0.5, rstd[:, :],
                                                   ALU.mult, ALU.mult))
                    chain(dve.scalar_tensor_tensor(rstd[:, :], newton[:, :], 1.5, rstd[:, :],
                                                   ALU.add, ALU.mult))
                for c in range(NC):
                    dve.tensor_scalar(xn[:, c, :], h[:, c, :], mv[:, c, 0:1], rstd[:, c:c + 1],
                                      ALU.subtract, ALU.mult).then_inc(ready, 1)

            for c in range(NC):
                dve.wait_ge(h_ready, c + 1)
                chain(dve.bn_stats(stats[:, c, :], h[:, c, :]))
            normalise(xn_ready)
            dve.wait_ge(xnT_ready, NC)
            for i in range(2):
                dve.tensor_copy(twice[:, :, :, i, :],
                                xnT[:, :, 0:N].rearrange("p k (b s) -> p k b s", s=S)).then_inc(twice_ready, 1)
            for j in range(2):
                dve.wait_ge(k_done, j + 1)
                for g in range(NKV):
                    dve.tensor_scalar(kbd[:, 8 * j:8 * j + 8, g, :],
                                      ps[:, 4 + j, 0:HALF].rearrange("p (b t) -> p b t", t=S),
                                      cst[:, C_GMASK + g:C_GMASK + g + 1], None, ALU.mult).then_inc(k_ready, 1)
            vmask = cst[0:MS, C_VMASK:C_VMASK + 2].unsqueeze(1)
            for j in range(2):
                dve.wait_ge(v_done, j + 1)
                dve.tensor_tensor(
                    vbd[:, 16 * j:16 * j + 16, :, 0:HD],
                    ps[0:MS, 6 + j, :].rearrange("p (b g d) -> p b g d", g=2, d=HD),
                    vmask.unsqueeze(3).to_broadcast([MS, 16, 2, HD]), ALU.mult).then_inc(v_ready, 1)
            dve.tensor_copy(vbd[:, :, :, HD], vmask.to_broadcast([MS, 2 * B, 2])).then_inc(v_ready, 1)

            def shift(i, par):
                sc = ps[0:MS, 2 * par:2 * par + 2, 0:IG * GT].rearrange("p m (g t) -> p m g t", t=S)
                dve.wait_ge(s_done, 2 * (i + 1))
                dve.tensor_reduce(top[:, par, :, :], sc, AX.X, ALU.max).then_inc(top_ready, 1)
                dve.wait_ge(top_ready, i + 1)
                if not (isinstance(i, int) and i < 2):
                    dve.wait_ge(pT_done, 2 * (i - 1))
                dve.tensor_tensor(prob[:, par, :, :, :], sc,
                                  top[:, par, :, :].unsqueeze(3).to_broadcast([MS, 2, IG * NKV, S]),
                                  ALU.subtract).then_inc(shifted, 1)

            def probs_out(i):
                dve.wait_ge(pT_done, 2 * i + 2)
                dve.tensor_copy(probT[:, 1, :], ps[0:MS, 5, 0:4 * MS]).then_inc(pT_odd, 1)

            def context(i):
                dve.wait_ge(c_done, i + 1)
                acc = ps[0:MS, 6, 0:IG * 4 * G2].rearrange("p (r d) -> p r d", d=HD + 1)
                dve.reciprocal(rsum[:, :], acc[:, :, HD]).then_inc(rsum_ready, 1)
                dve.wait_ge(rsum_ready, i + 1)
                dve.tensor_tensor(ctxn[:, :, :].rearrange("p b (r d) -> p (b r) d", d=HD), acc[:, :, 0:HD],
                                  rsum[:, :].unsqueeze(2).to_broadcast([MS, 4 * NKV, HD]),
                                  ALU.mult).then_inc(ctxn_ready, 1)

            shift(0, 0)
            shift(1, 1)
            with dve.Fori(0, NG // 2 - 1) as k:
                for i in range(2):
                    probs_out(2 * k + i)
                    context(2 * k + i)
                    shift(2 * k + i + 2, i)
            for i in range(NG - 2, NG):
                probs_out(i)
                context(i)

            for c in range(NC):
                dve.wait_ge(wo_done, c + 1)
                if c == 0:
                    dve.wait_ge(xnT_done, NC)
                chain(dve.tensor_tensor(h[:, c, :], h[:, c, :], ps[:, c, 0:D], ALU.add))
                chain(dve.bn_stats(stats[:, c, :], h[:, c, :]))
            normalise(xn2_ready)

            def over_experts(ap):
                return ap.unsqueeze(2).to_broadcast([P, NC, E])

            rev = cst[:, C_REVERSED:C_REVERSED + E].unsqueeze(1).to_broadcast([P, NC, E])

            def pick(j, src):
                chain(dve.tensor_reduce(mx[:, j, :], src, AX.X, ALU.max))
                chain(dve.tensor_tensor(eq[:, :, :], src, over_experts(mx[:, j, :]), ALU.is_equal))
                chain(dve.tensor_tensor(eq[:, :, :], eq[:, :, :], rev, ALU.mult))
                chain(dve.tensor_reduce(rv[:, :], eq[:, :, :], AX.X, ALU.max))
                chain(dve.tensor_tensor(mask[:, j, :, :], rev, over_experts(rv[:, :]), ALU.is_equal))

            dve.wait_ge(logits_done, 1)
            chain(dve.tensor_copy(lg[:, :, :], ps[:, 7, 0:NC * E].rearrange("p (c e) -> p c e", e=E)))
            pick(0, lg[:, :, :])
            dve.tensor_tensor(ex[:, :, :], lg[:, :, :], over_experts(mx[:, 0, :]),
                              ALU.subtract).then_inc(logit_shift, 1)
            chain(dve.scalar_tensor_tensor(lg2[:, :, :], mask[:, 0, :, :], NEG, lg[:, :, :], ALU.mult, ALU.add))
            pick(1, lg2[:, :, :])
            chain(dve.tensor_tensor(eq[:, :, :], mask[:, 0, :, :], mask[:, 1, :, :], ALU.add))
            dve.tensor_tensor(both[:, :, :], eq[:, :, :], over_experts(cst[:, C_VALID:C_VALID + NC]),
                              ALU.mult).then_inc(both_ready, 1)
            dve.wait_ge(ex_ready, 1)
            chain(dve.tensor_reduce(den[:, :], ex[:, :, :], AX.X, ALU.add))
            chain(dve.reciprocal(den[:, :], den[:, :]))
            for j in range(TOPK):
                chain(dve.tensor_tensor(lg[:, :, :], ex[:, :, :], mask[:, j, :, :], ALU.mult))
                chain(dve.tensor_reduce(gate[:, j, :], lg[:, :, :], AX.X, ALU.add))
                chain(dve.tensor_tensor(gate[:, j, :], gate[:, j, :], den[:, :], ALU.mult))
            dve.wait_ge(count_done, 1)
            chain(dve.memset(count[:, 0, :], 0.0))
            for c in range(NC):
                chain(dve.tensor_tensor(count[:, c + 1, :], count[:, c, :], ps[:, 6, c * E:c * E + E], ALU.add))
            chain(dve.tensor_scalar(over[:, :, :].rearrange("p e c -> p c e"),
                                    cst[:, C_TILE:C_TILE + NC].unsqueeze(2).to_broadcast([P, NC, E]),
                                    float(P), None, ALU.mult))
            chain(dve.tensor_tensor(over[:, :, :], count[:, NC, :].unsqueeze(2).to_broadcast([P, E, NC]),
                                    over[:, :, :], ALU.is_gt))
            chain(dve.tensor_reduce(used[:, :], over[:, :, :], AX.X, ALU.add))
            chain(dve.tensor_tensor_scan(end[:, :], ones8[:, :], used[:, :], 0.0, ALU.mult, ALU.add))
            chain(dve.tensor_tensor(start[:, :], end[:, :], used[:, :], ALU.subtract))
            chain(dve.tensor_tensor(rank[:, :, :], count[:, 0:NC, :],
                                    ps[:, 5, 0:NC * E].rearrange("p (c e) -> p c e", e=E), ALU.add))
            chain(dve.scalar_tensor_tensor(slot_e[:, :, :], start[:, :].unsqueeze(1).to_broadcast([P, NC, E]),
                                           float(P), rank[:, :, :], ALU.mult, ALU.add))
            for j in range(TOPK):
                chain(dve.tensor_tensor(lg2[:, :, :], slot_e[:, :, :], mask[:, j, :, :], ALU.mult))
                chain(dve.tensor_reduce(slot_f[:, j, :], lg2[:, :, :], AX.X, ALU.add))
            dve.tensor_copy(slot[:, :, :], slot_f[:, :, :]).then_inc(slots_ready, 1)
            chain(dve.tensor_tensor(le[:, :, :], end[:, :].unsqueeze(1).to_broadcast([P, TILES, E]),
                                    cst[:, C_TILE:C_TILE + TILES].unsqueeze(2).to_broadcast([P, TILES, E]),
                                    ALU.is_le))
            chain(dve.tensor_reduce(eid_f[:, :], le[:, :, :], AX.X, ALU.add))
            dve.tensor_scalar(eid[:, :], eid_f[:, :], float(E - 1), None, ALU.min).then_inc(eid_ready, 1)

            def rows_T(t, i):
                dve.wait_ge(xT_done, t + 1)
                dve.tensor_copy(x_T[:, i, :], ps[:, 4, 0:D]).then_inc(xT_ready, 1)

            def hidden_T(t):
                for q in range(2):
                    dve.wait_ge(hT_done, 2 * t + q + 1)
                    dve.tensor_copy(hidT[:, 4 * q:4 * q + 4, :],
                                    ps[:, 2 + q, :].rearrange("p (k n) -> p k n", n=P)).then_inc(hT_ready, 1)

            def result(t, i):
                dve.wait_ge(y_done, t + 1)
                if not (isinstance(t, int) and t < 2):
                    dve.wait_ge(y_out[i], 8 * (t - i))
                dve.tensor_copy(y_sb[:, i, :], ps[:, 5, 0:D]).then_inc(y_ready, 1)

            rows_T(0, 0)
            rows_T(1, 1)
            for t in range(2):
                hidden_T(t)
                rows_T(t + 2, t)
                result(t, t)
            with dve.Fori(1, (TILES - 3) // 2) as k:
                for i in range(2):
                    hidden_T(2 * k + i)
                    rows_T(2 * k + i + 2, i)
                    result(2 * k + i, i)
            hidden_T(TILES - 3)
            rows_T(TILES - 1, 0)
            result(TILES - 3, 0)
            for t in range(TILES - 2, TILES):
                hidden_T(t)
                result(t, t % 2)

            for c in range(NC):
                n = P if c < NC - 1 else LAST
                dve.wait_ge(picked_in, 16 * TOPK * (c + 1) if c == NC - 1 else 16 * TOPK * NC)
                chain(dve.scalar_tensor_tensor(h[0:n, c, :], picked[0:n, c * TOPK, :], gate[0:n, 0, c:c + 1],
                                               h[0:n, c, :], ALU.mult, ALU.add))
                dve.scalar_tensor_tensor(h[0:n, c, :], picked[0:n, c * TOPK + 1, :], gate[0:n, 1, c:c + 1],
                                         h[0:n, c, :], ALU.mult, ALU.add).then_inc(out_ready, 1)

        @block.tensor
        def _(pe):
            pe.wait_ge(pos_in, 64)
            for c in range(NC):
                pe.matmul(ps[:, c, 0:D], pos_rows_sb[:, c * P:(c + 1) * P], pos_sb[:, :], start=True, stop=False)
            for k in range(KP):
                if k % 2 == 0:
                    pe.wait_ge(patch_in[k // 2], 32)
                for c in range(NC):
                    mm = pe.matmul(ps[:, c, 0:D], patches_sb[:, k, c * P:(c + 1) * P], w_tok_sb[:, k, :],
                                   start=False, stop=(k == KP - 1))
                    if k == KP - 1:
                        mm.then_inc(tok_done, 1)
            pe.wait_ge(const_in, 16)
            for c in range(NC):
                pe.wait_ge(xn_ready, c + 1)
                if c >= 3:
                    pe.wait_ge(xnT_ready, c - 2)
                for k in range(KD):
                    mm = pe.transpose(ps[:, 5 + c % 3, k * P:(k + 1) * P], xn[:, c, k * P:(k + 1) * P], ident)
                mm.then_inc(xnT_done, 1)
            pe.wait_ge(attn_in, 96)
            pe.wait_ge(xnT_ready, NC)
            pe.wait_ge(h_ready, NC)
            for j in range(2):
                for k in range(KD):
                    mm = pe.matmul(ps[:, 4 + j, 0:HALF], wk_sb[:, k, :, :].rearrange("p i f -> p (i f)"),
                                   xnT[:, k, j * HALF:(j + 1) * HALF], start=(k == 0), stop=(k == KD - 1))
                mm.then_inc(k_done, 1)
            for m in range(2):
                for j in range(2):
                    for k in range(KD):
                        mm = pe.matmul(ps[:, 2 * m + j, 0:HALF], wq_sb[:, k, m, :],
                                       xnT[:, k, j * HALF:(j + 1) * HALF], start=(k == 0), stop=(k == KD - 1))
                    mm.then_inc(q_done, 1)
            pe.wait_ge(twice_ready, 2)
            for b in range(B):
                for k in range(KD):
                    mm = pe.matmul(ps[0:MS, 6 + b // 8, (b % 8) * 64:(b % 8) * 64 + 64],
                                   twice[:, k, b, :, :].rearrange("p i s -> p (i s)"), wv_sb[:, k, :],
                                   start=(k == 0), stop=(k == KD - 1))
                if b % 8 == 7:
                    mm.then_inc(v_done, 1)

            def scores(i, par, m):
                pe.wait_ge(staged, 2 * (i + 1))
                for b in range(IG):
                    dst = ps[0:MS, 2 * par + m, b * GT:(b + 1) * GT]
                    pe.matmul(dst, ident_bf[0:MS, 0:MS], amask[0:MS, :], start=True, stop=False)
                    mm = pe.matmul(dst, q_st[m * 64:m * 64 + 64, par, b * MS:(b + 1) * MS],
                                   k_st[m * 64:m * 64 + 64, par, b * GT:(b + 1) * GT], start=False, stop=True)
                mm.then_inc(s_done, 1)

            def attend(i, par, more):
                pe.wait_ge(p_ready, i + 1)
                if not (isinstance(i, int) and i == 0):
                    pe.wait_ge(pT_even, i)
                    pe.wait_ge(pT_odd, i)
                for b in range(IG):
                    for m in range(2):
                        for g in range(2):
                            n = (2 * m + g) * MS
                            src = prob[:, par, m, b * NKV + 2 * g:b * NKV + 2 * g + 2, :]
                            mm = pe.transpose(ps[0:MS, 4 + b, n:n + MS], src.rearrange("p g t -> p (g t)"),
                                              ident[0:MS, 0:MS])
                    mm.then_inc(pT_done, 1)
                if more:
                    pe.wait_ge(shifted, i + 1)
                    scores(i + 2, par, 0)
                if not (isinstance(i, int) and i == 0):
                    pe.wait_ge(ctxn_ready, i)
                for b in range(IG):
                    pe.wait_ge((pT_even, pT_odd)[b], i + 1)
                    for m in range(2):
                        for g in range(2):
                            r = (b * 2 + m) * 2 + g
                            mm = pe.matmul(ps[0:MS, 6, r * G2:(r + 1) * G2],
                                           probT[:, b, (2 * m + g) * MS:(2 * m + g + 1) * MS],
                                           vbd[:, :, :, :].rearrange("p r g d -> p (r g d)")
                                           [:, bass.ds(((i * IG + b) * 2 + g) * G2, G2)], start=True, stop=True)
                mm.then_inc(c_done, 1)
                if more:
                    scores(i + 2, par, 1)
                pe.wait_ge(ctxn_ready, i + 1)
                if not (isinstance(i, int) and i == 0):
                    pe.wait_ge(ctxT_ready, i)
                for b in range(IG):
                    mm = pe.transpose(ps[:, 7, b * MS:(b + 1) * MS], ctxn[:, b, :], ident[0:MS, 0:MS])
                mm.then_inc(cT_done, 1)

            pe.wait_ge(const_ready, 5)
            pe.wait_ge(v_ready, 3)
            for i in range(2):
                for m in range(2):
                    scores(i, i, m)
            for i in range(2):
                attend(i, i, True)
            with pe.Fori(1, NG // 2 - 1) as k:
                for i in range(2):
                    attend(2 * k + i, i, True)
            for i in range(NG - 2, NG):
                attend(i, i % 2, False)

            pe.wait_ge(ctxT_ready, NG)
            pe.wait_ge(cleared, 2)
            for c in range(NC):
                for m in range(2):
                    mm = pe.matmul(ps[:, c, 0:D], ctxT[:, m, c * P:(c + 1) * P], wo_sb[:, m, :],
                                   start=(m == 0), stop=(m == 1))
                mm.then_inc(wo_done, 1)

            def route(c):
                pe.wait_ge(xn2T_ready, c + 1)
                for k in range(KD):
                    mm = pe.matmul(ps[:, 7, c * E:(c + 1) * E], xnT[:, k, c * P:(c + 1) * P], wr_sb[:, k, :],
                                   start=(k == 0), stop=(k == KD - 1))
                if c == NC - 1:
                    mm.then_inc(logits_done, 1)

            for c in range(NC):
                pe.wait_ge(xn2_ready, c + 1)
                if c >= 2:
                    pe.wait_ge(xn2T_ready, c - 1)
                for k in range(KD):
                    mm = pe.transpose(ps[:, 5 + c % 2, k * P:(k + 1) * P], xn[:, c, k * P:(k + 1) * P], ident)
                mm.then_inc(xn2T_done, 1)
                if c >= 1:
                    route(c - 1)
            route(NC - 1)
            pe.wait_ge(both_ready, 1)
            chosen = both[:, :, :].rearrange("p c e -> p (c e)")
            pe.matmul(ps[:, 5, 0:NC * E], upper_bf[:, :], chosen, start=True, stop=True)
            pe.matmul(ps[:, 6, 0:NC * E], ones_bf[:, :], chosen, start=True, stop=True).then_inc(count_done, 1)

            def expert(t):
                return pe.value_load(eid[0:1, bass.ds(t, 1)], min_val=0, max_val=E - 1)

            def rows_T(t, i, k):
                pe.wait_ge(x_in[i], 16 * k)
                if not (isinstance(t, int) and t == 0):
                    pe.wait_ge(xT_ready, t)
                for q in range(KD):
                    mm = pe.transpose(ps[:, 4, q * P:(q + 1) * P], x_sb[:, i, q * P:(q + 1) * P], ident)
                mm.then_inc(xT_done, 1)

            def up(t, i, e, half):
                if half == 0:
                    pe.wait_ge(xT_ready, t + 1)
                if not (isinstance(t, int) and t == 0):
                    pe.wait_ge(hid_ready, 2 * t - 1 + half)
                for k in range(KD):
                    mm = pe.matmul(ps[:, half, :], x_T[:, i, k * P:(k + 1) * P],
                                   wi_sb[:, bass.ds(e * (KD * F) + k * F + half * 512, 512)],
                                   start=(k == 0), stop=(k == KD - 1))
                mm.then_inc(up_done, 1)

            def hidden_T(t, i):
                pe.wait_ge(hid_ready, 2 * t + 2)
                if not (isinstance(t, int) and t == 0):
                    pe.wait_ge(hT_ready, 2 * t)
                for q in range(2):
                    for k in range(4):
                        mm = pe.transpose(ps[:, 2 + q, k * P:(k + 1) * P], hid[:, i, 4 * q + k, :], ident)
                    mm.then_inc(hT_done, 1)

            def down(t, e):
                if not (isinstance(t, int) and t == 0):
                    pe.wait_ge(y_ready, t)
                for k in range(FC):
                    if k % 4 == 0:
                        pe.wait_ge(hT_ready, 2 * t + 1 + k // 4)
                    mm = pe.matmul(ps[:, 5, 0:D], hidT[:, k, :], w2_sb[:, bass.ds(e * (FC * D) + k * D, D)],
                                   start=(k == 0), stop=(k == FC - 1))
                mm.then_inc(y_done, 1)

            def tile(t, i, k, e, e_next, ahead):
                if e_next is not None:
                    up(t + 1, 1 - i, e_next, 0)
                hidden_T(t, i)
                if ahead:
                    rows_T(t + 2, i, k + 2)
                if e_next is not None:
                    up(t + 1, 1 - i, e_next, 1)
                down(t, e)

            pe.wait_ge(ffn_in, 16 * 2 * E)
            pe.wait_ge(eid_ready, 1)
            rows_T(0, 0, 1)
            rows_T(1, 1, 1)
            first = expert(0)
            for half in range(2):
                up(0, 0, first, half)
            second, third = expert(1), expert(2)
            tile(0, 0, 0, first, second, True)
            tile(1, 1, 0, second, third, True)
            with pe.Fori(1, (TILES - 3) // 2) as k:
                experts = [expert(2 * k + i) for i in range(3)]
                for i in range(2):
                    tile(2 * k + i, i, k, experts[i], experts[i + 1], True)
            k = (TILES - 3) // 2
            last = [expert(2 * k + i) for i in range(3)]
            tile(TILES - 3, 0, k, last[0], last[1], True)
            tile(TILES - 2, 1, k, last[1], last[2], False)
            tile(TILES - 1, 0, k, last[2], None, False)


def kernel(x, L0_tok_W, L0_tok_b, L0_tok_cls_token, L0_tok_pos_embedding, L0_attn_wq, L0_attn_wk, L0_attn_wv,
           L0_attn_wo, L0_ffn_w_router, L0_ffn_wi, L0_ffn_wo):
    import concourse.bacc as bacc
    from concourse.bass_utils import run_bass_kernel_spmd

    def rows(a, *shape):
        return np.ascontiguousarray(a.reshape(shape))

    x, w, wq, wk, wv, wo = (np.asarray(a) for a in (x, L0_tok_W, L0_attn_wq, L0_attn_wk, L0_attn_wv, L0_attn_wo))
    patches = np.zeros((C * PATCH * PATCH, NP), x.dtype)
    patches[:, :N].reshape(-1, B, S)[:, :, 1:] = \
        x.reshape(B, C, GRID, PATCH, GRID, PATCH).transpose(1, 3, 5, 0, 2, 4).reshape(-1, B, S - 1)

    def by_partition(a):
        return np.ascontiguousarray(a.reshape(a.shape[0] // P, P, -1).transpose(1, 0, 2))

    q = wq.T.reshape(D, NKV, 2, 2, HD).transpose(0, 3, 2, 1, 4).reshape(KD, P, 2, P).transpose(1, 0, 2, 3)
    o = wo.T.reshape(NKV, 2, 2, HD, D).transpose(2, 1, 0, 3, 4).reshape(2, P, D).transpose(1, 0, 2)
    arrays = {
        "patches": by_partition(patches), "w_tok": by_partition(w.T), "bias": np.asarray(L0_tok_b),
        "cls": np.asarray(L0_tok_cls_token), "pos": np.asarray(L0_tok_pos_embedding),
        "wq": np.ascontiguousarray(q), "wk": by_partition(wk.T), "wv": by_partition(wv.T),
        "wo": np.ascontiguousarray(o), "w_router": np.asarray(L0_ffn_w_router),
        "wi": np.asarray(L0_ffn_wi), "w2": np.asarray(L0_ffn_wo),
        "consts": constants(), "pos_rows": position_rows(),
    }
    nc = bacc.Bacc("TRN2", target_bir_lowering=False, num_devices=1)
    args = [nc.dram_tensor(f"in_{n}", a.shape, mybir.dt.from_np(a.dtype), kind="ExternalInput").ap()
            for n, a in arrays.items()]
    out = nc.dram_tensor("out", (N, D), F32, kind="ExternalOutput").ap()
    vit_block(nc, *args, out)
    r = run_bass_kernel_spmd(nc, [{f"in_{n}": a for n, a in arrays.items()}], core_ids=[0])
    return r.results[0]["out"].reshape(B, S, D)
```

```python
from contextlib import ExitStack

import numpy as np

import concourse.bass as bass
from concourse import mybir

F32 = mybir.dt.float32
BF16 = mybir.dt.bfloat16
I32 = mybir.dt.int32
U32 = mybir.dt.uint32
ALU = mybir.AluOpType
ACT = mybir.ActivationFunctionType
AX = mybir.AxisListType

P = 128
B, C, IMG, PATCH, D = 16, 3, 96, 16, 256
GRID = IMG // PATCH
S = GRID * GRID + 1
N = B * S
NC = -(-N // P)
LAST = N - (NC - 1) * P
KP = C * PATCH * PATCH // P
KD = D // P
NKV, GS, HD = 4, 4, 16
GT = NKV * S
MS = 2 * S
G2 = 2 * (HD + 1)
IG = 2
NG = B // IG
BH = B // 2
HALF = N // 2
E, F, TOPK = 8, 1024, 2
FC = F // P
CAP = 192
CR = CAP // 2
BLOCKS = -(-N // CAP)
EROWS = BLOCKS * CAP
EPS = 1e-5
NEG = -1e30


def most_tiles_over():
    best = np.zeros(N * TOPK + 1, int)
    for _ in range(E):
        nxt = best.copy()
        for extra in range(1, BLOCKS):
            need = CAP * extra + 1
            nxt[need:] = np.maximum(nxt[need:], best[:-need] + extra)
        best = nxt
    return int(best[-1])


OVER = most_tiles_over()
OVER += OVER % 2
T_END = E + OVER
ROWS = E * EROWS + (OVER + 1) * CAP

EXTRA = {
    (2, "a"): [("W", 0)], (3, "a"): [("X", 0)], (3, "b"): [("R", 0)], (4, "a"): [("K", 0)],
    (4, "b"): [("W", 1)], (5, "a"): [("X", 1)], (5, "b"): [("R", 1)], (6, "a"): [("W", 2), ("K", 1)],
    (6, "b"): [("X", 2)], (7, "a"): [("W", 3), ("R", 2)],
    (7, "b"): [("W", 4), ("K", 2), ("X", 3), ("R", 3), ("X", 4), ("K", 3), ("R", 4), ("K", 4)],
}
CHUNK_BANK = [7, 7, 0, 1, 7]

C_IDENT = 0
C_AMASK = C_IDENT + P
C_GMASK = C_AMASK + GT
C_VMASK = C_GMASK + NKV
C_UPPER = C_VMASK + 2
C_EXPERT = C_UPPER + P
C_BASE = C_EXPERT + E
C_LIMIT = C_BASE + E
C_TILE = C_LIMIT + BLOCKS - 1
C_END = C_TILE + OVER


def constants():
    c = np.zeros((P, C_END), np.float32)
    p = np.arange(P)
    c[:, C_IDENT:C_IDENT + P] = np.eye(P)
    c[:, C_AMASK:C_AMASK + GT] = np.where(np.arange(GT)[None] % S > p[:, None] % S, NEG, 0.0)
    c[:, C_GMASK:C_GMASK + NKV] = (p[:, None] % (NKV * HD)) // HD == np.arange(NKV)[None]
    c[:, C_VMASK:C_VMASK + 2] = p[:, None] // S == np.arange(2)[None]
    c[:, C_UPPER:C_UPPER + P] = p[:, None] < p[None]
    c[:, C_EXPERT:C_EXPERT + E] = np.arange(E)[None]
    c[:, C_BASE:C_BASE + E] = np.arange(E)[None] * EROWS
    c[:, C_LIMIT:C_LIMIT + BLOCKS - 1] = np.arange(1, BLOCKS)[None] * CAP
    c[:, C_TILE:C_TILE + OVER] = np.arange(OVER)[None]
    return c


def position_rows():
    n = np.arange(N)
    rows = np.zeros((S + 2, N), np.float32)
    for s in range(S):
        rows[s] = n % S == s
    rows[S] = n % S != 0
    rows[S + 1] = n % S == 0
    return rows


def rows_of(c):
    return P if c < NC - 1 else LAST


def images_of(c):
    return -(-(c * P + rows_of(c)) // (IG * S))


def vit_block(nc, patches, w_tok, bias, cls, pos, wq, wk, wv, wo, w_router, wi, w2, consts, pos_rows, out):
    ctx = ExitStack()
    with ctx:
        def sb(name, shape, dt=F32):
            return ctx.enter_context(nc.sbuf_tensor(name, shape, dt))

        def sem(name):
            return ctx.enter_context(nc.semaphore(name))

        rows = nc.dram_tensor("rows", [ROWS, D], F32, kind="Internal").ap()

        patches_sb = sb("patches_sb", [P, KP, N])
        w_tok_sb = sb("w_tok_sb", [P, KP, D])
        pos_rows_sb = sb("pos_rows_sb", [S + 2, N])
        pos_sb = sb("pos_sb", [S + 2, D])
        cst = sb("cst", [P, C_END])
        wq_sb = sb("wq_sb", [P, KD, 2, P])
        wk_sb = sb("wk_sb", [P, KD, 2, NKV * HD])
        wv_sb = sb("wv_sb", [P, KD, NKV * HD])
        wo_sb = sb("wo_sb", [P, 2, D])
        wr_sb = sb("wr_sb", [P, KD, E])
        amask = sb("amask", [P, GT], BF16)
        ident_bf = sb("ident_bf", [P, P], BF16)
        upper_bf = sb("upper_bf", [P, P], BF16)
        ones_bf = sb("ones_bf", [P, P], BF16)
        half = sb("half", [P, 1])
        zeros = sb("zeros", [CR, 2 * D])
        h = sb("h", [P, NC, D])
        xn = sb("xn", [P, NC, D])
        xnT = sb("xnT", [P, KD, N])
        stats = sb("stats", [P, NC, 6])
        mv = sb("mv", [P, NC, 2])
        var = sb("var", [P, NC, 2])
        root = sb("root", [P, NC])
        newton = sb("newton", [P, NC])
        rstd = sb("rstd", [P, NC])
        twice = sb("twice", [P, KD, B, 2, S])
        qT = sb("qT", [P, B, 2, S])
        kbd = sb("kbd", [P, B, NKV, S])
        vbd = sb("vbd", [MS, B * 2, 2, HD + 1])
        top = sb("top", [MS, 2, 2, IG * NKV])
        prob = sb("prob", [MS, 2, 2, IG * NKV, S])
        probT = sb("probT", [MS, IG, 4 * MS])
        rsum = sb("rsum", [MS, 4 * NKV])
        ctxn = sb("ctxn", [MS, IG, 2 * NKV * HD])
        ctxT = sb("ctxT", [P, 2, N])
        lg = sb("lg", [P, NC, E])
        best = sb("best", [P, NC, 8])
        best_at = sb("best_at", [P, NC, 8], U32)
        neg_top = sb("neg_top", [P, NC])
        ex = sb("ex", [P, NC, 8])
        den = sb("den", [P, NC])
        gate = sb("gate", [P, NC, TOPK])
        mask = sb("mask", [P, NC, TOPK, E])
        both = sb("both", [P, NC, E], BF16)
        place = sb("place", [P, NC, E])
        place_k = sb("place_k", [P, NC, TOPK, E])
        slot_f = sb("slot_f", [P, NC, TOPK])
        slot = sb("slot", [P, NC, TOPK], I32)
        beyond = sb("beyond", [1, E, BLOCKS - 1])
        used = sb("used", [1, E])
        end = sb("end", [1, E])
        ended = sb("ended", [1, OVER, E])
        begun = sb("begun", [1, OVER, E])
        o_expert = sb("o_expert", [1, OVER])
        o_block = sb("o_block", [1, OVER])
        o_row = sb("o_row", [1, OVER])
        over_tab = sb("over_tab", [1, 2, OVER], I32)
        over_any = sb("over_any", [1, 1], I32)
        wi_sb = sb("wi_sb", [P, 2, KD, F])
        w2_sb = sb("w2_sb", [P, 2, FC, D])
        x_sb = sb("x_sb", [CR, 2, D])
        x_T = sb("x_T", [P, KD, CAP])
        hidT = sb("hidT", [P, FC, CAP])
        yT = sb("yT", [P, KD, CAP])
        y_sb = sb("y_sb", [CR, 2, D])
        picked = sb("picked", [P, NC * TOPK, D])

        ident = cst[:, C_IDENT:C_IDENT + P]

        ps = ctx.enter_context(nc.psum_tensor("ps", [P, 8, 512], F32))
        UP, DOWN, XT, YO = 0, 4, 6, 7

        pos_in = sem("pos_in")
        patch_in = [sem(f"patch_in{i}") for i in range(KP // 2)]
        const_in = sem("const_in")
        attn_in = sem("attn_in")
        wi_in = [sem(f"wi_in{i}") for i in range(2)]
        w2_in = [sem(f"w2_in{i}") for i in range(2)]
        cleared = sem("cleared")
        zero_rows = sem("zero_rows")
        const_ready = sem("const_ready")
        tok_done = sem("tok_done")
        h_ready = sem("h_ready")
        stats_ready = sem("stats_ready")
        xn_ready = sem("xn_ready")
        xnT_done = sem("xnT_done")
        xnT_ready = sem("xnT_ready")
        twice_ready = sem("twice_ready")
        q_done = sem("q_done")
        q_ready = sem("q_ready")
        k_done = sem("k_done")
        k_ready = sem("k_ready")
        v_done = sem("v_done")
        v_ready = sem("v_ready")
        s_done = sem("s_done")
        top_ready = sem("top_ready")
        shifted = sem("shifted")
        p_ready = sem("p_ready")
        pT_done = sem("pT_done")
        pT_ready = sem("pT_ready")
        c_done = sem("c_done")
        rsum_ready = sem("rsum_ready")
        ctxn_ready = sem("ctxn_ready")
        cT_done = sem("cT_done")
        ctxT_ready = sem("ctxT_ready")
        wo_done = sem("wo_done")
        stats2_ready = sem("stats2_ready")
        xn2_ready = sem("xn2_ready")
        xn2T_done = sem("xn2T_done")
        xn2T_ready = sem("xn2T_ready")
        logits_done = sem("logits_done")
        neg_ready = sem("neg_ready")
        ex_ready = sem("ex_ready")
        both_ready = sem("both_ready")
        rank_done = sem("rank_done")
        place_ready = sem("place_ready")
        slots_ready = sem("slots_ready")
        over_ready = sem("over_ready")
        scattered = sem("scattered")
        x_in = sem("x_in")
        xT_done = sem("xT_done")
        xT_ready = sem("xT_ready")
        up_done = sem("up_done")
        hid_ready = sem("hid_ready")
        down_done = sem("down_done")
        yT_ready = sem("yT_ready")
        yo_done = sem("yo_done")
        y_ready = sem("y_ready")
        y_out = sem("y_out")
        picked_in = [sem(f"picked_in{c}") for c in range(NC)]
        out_ready = sem("out_ready")
        out_sent = sem("out_sent")
        step = sem("step")
        pool_step = sem("pool_step")

        block = ctx.enter_context(nc.Block())

        def over(eng):
            eng.wait_ge(over_ready, 1)
            return eng.value_load(over_any[0:1, 0:1], min_val=0, max_val=OVER) > 0

        @block.sync
        def _(sp):
            sp.dma_start(pos_rows_sb[:, :], pos_rows).then_inc(pos_in, 16)
            sp.dma_start(pos_sb[0:S, :], pos[0, :, :]).then_inc(pos_in, 16)
            sp.dma_start(pos_sb[S:S + 1, :], bias.rearrange("(a d) -> a d", a=1)).then_inc(pos_in, 16)
            sp.dma_start(pos_sb[S + 1:S + 2, :], cls[0, :, :]).then_inc(pos_in, 16)
            for i in range(KP // 2):
                k = slice(2 * i, 2 * i + 2)
                sp.dma_start(w_tok_sb[:, k, :], w_tok[:, k, :]).then_inc(patch_in[i], 16)
                sp.dma_start(patches_sb[:, k, :], patches[:, k, :]).then_inc(patch_in[i], 16)
            sp.dma_start(cst[:, :], consts).then_inc(const_in, 16)
            for i in range(2):
                sp.dma_start(wk_sb[:, :, i, :], wk).then_inc(attn_in, 16)
            sp.dma_start(wq_sb[:, :, :, :], wq).then_inc(attn_in, 16)
            sp.dma_start(wv_sb[:, :, :], wv).then_inc(attn_in, 16)
            sp.dma_start(wo_sb[:, :, :], wo).then_inc(attn_in, 16)
            sp.dma_start(wr_sb[:, :, :], w_router.rearrange("(k p) e -> p k e", p=P)).then_inc(attn_in, 16)
            sp.wait_ge(cleared, 1)
            sp.dma_start(rows.rearrange("(n p r) d -> p n (r d)", p=CR, r=2),
                         zeros[:, :].unsqueeze(1).to_broadcast([CR, ROWS // CAP, 2 * D])).then_inc(zero_rows, 16)

            def load_wi(e, i):
                sp.dma_start(wi_sb[:, i, :, :],
                             wi[bass.ds(e, 1), :, :].rearrange("a (k p) f -> p (a k) f", p=P)
                             ).then_inc(wi_in[i], 16)

            def load_w2(e, i):
                sp.dma_start(w2_sb[:, i, :, :].rearrange("p k d -> p (k d)"),
                             w2[bass.ds(e, 1), :, :].rearrange("a (p k) d -> p (a k d)", p=P)
                             ).then_inc(w2_in[i], 16)

            def load_x(row):
                sp.dma_start(x_sb[:, :, :], rows[bass.ds(row, CAP), :].rearrange("(p r) d -> p r d", r=2)
                             ).then_inc(x_in, 16)

            def store_y(t, row):
                sp.wait_ge(y_ready, t + 1)
                sp.dma_start(rows[bass.ds(row, CAP), :].rearrange("(p r) d -> p r d", r=2), y_sb[:, :, :]
                             ).then_inc(y_out, 16)

            def tile(t, i, row, next_row, e_after):
                if next_row is not None:
                    sp.wait_ge(xT_done, t + 1)
                    load_x(next_row)
                if e_after is not None:
                    sp.wait_ge(up_done, FC // 2 * (t + 1))
                    load_wi(e_after, i)
                    sp.wait_ge(down_done, t + 1)
                    load_w2(e_after, i)
                store_y(t, row)

            for i in range(2):
                load_wi(i, i)
                load_w2(i, i)
            sp.wait_ge(scattered, 16 * TOPK * NC)
            load_x(0)
            with sp.Fori(0, E // 2 - 1) as k:
                for i in range(2):
                    t = 2 * k + i
                    tile(t, i, t * EROWS, (t + 1) * EROWS, t + 2)
            tile(E - 2, 0, (E - 2) * EROWS, (E - 1) * EROWS, None)
            tile(E - 1, 1, (E - 1) * EROWS, None, None)

            with sp.If(over(sp)):
                def expert(t):
                    return sp.value_load(over_tab[0:1, 0, bass.ds(t - E, 1)], min_val=0, max_val=E - 1)

                def row(t):
                    return sp.value_load(over_tab[0:1, 1, bass.ds(t - E, 1)],
                                         min_val=0, max_val=ROWS - CAP)

                for i in range(2):
                    e = expert(E + i)
                    load_wi(e, i)
                    load_w2(e, i)
                load_x(row(E))
                with sp.Fori(E // 2, T_END // 2 - 1) as k:
                    for i in range(2):
                        t = 2 * k + i
                        tile(t, i, row(t), row(t + 1), expert(t + 2))
                tile(T_END - 2, 0, row(T_END - 2), row(T_END - 1), None)
                tile(T_END - 1, 1, row(T_END - 1), None, None)

            for c in range(NC):
                n = rows_of(c)
                sp.wait_ge(out_ready, c + 1)
                sp.dma_start(out[c * P:c * P + n, :], h[0:n, c, :]).then_inc(out_sent, 16)
            sp.wait_ge(out_sent, 16 * NC)

        @block.gpsimd
        def _(pool):
            steps = [0]

            def chain(ins):
                steps[0] += 1
                ins.then_inc(pool_step, 1)
                pool.wait_ge(pool_step, steps[0])

            pool.memset(zeros[:, :], 0.0).then_inc(cleared, 1)
            chain(pool.memset(half[:, :], -0.5))

            def normalise(c, ready):
                n = rows_of(c)
                v, r, w = var[0:n, c, :], root[0:n, c:c + 1], newton[0:n, c:c + 1]
                pool.tensor_scalar(v[:, 1:2], mv[0:n, c, 1:2], EPS, -0.5, ALU.add, ALU.mult)
                chain(pool.tensor_scalar(v[:, 0:1], mv[0:n, c, 1:2], EPS, None, ALU.add))
                chain(pool.tensor_tensor(r, v[:, 0:1], half[0:n, :], ALU.pow))
                chain(pool.tensor_scalar(w, r, v[:, 1:2], r, ALU.mult, ALU.mult))
                chain(pool.tensor_scalar(rstd[0:n, c:c + 1], w, 1.5, r, ALU.add, ALU.mult))
                pool.tensor_scalar(xn[0:n, c, :], h[0:n, c, :], mv[0:n, c, 0:1], rstd[0:n, c:c + 1],
                                   ALU.subtract, ALU.mult).then_inc(ready, 1)

            def scatter(c):
                n = rows_of(c)
                pool.wait_ge(slots_ready, c + 1)
                for j in range(TOPK):
                    pool.indirect_dma_start(
                        out=rows, out_offset=bass.IndirectOffsetOnAxis(ap=slot[0:n, c, j:j + 1], axis=0),
                        in_=xn[0:n, c, :], in_offset=None).then_inc(scattered, 16)

            for c in range(NC):
                pool.wait_ge(stats_ready, c + 1)
                normalise(c, xn_ready)

            def second_norm(c):
                pool.wait_ge(stats2_ready, c + 1)
                pool.wait_ge(xnT_done, NC)
                normalise(c, xn2_ready)

            second_norm(0)
            pool.wait_ge(zero_rows, 16)
            scatter(0)
            second_norm(1)
            second_norm(2)
            scatter(1)
            second_norm(3)
            second_norm(4)
            for c in range(2, NC):
                scatter(c)

            pool.wait_ge(y_out, 16 * E)
            with pool.If(over(pool)):
                pool.wait_ge(y_out, 16 * T_END)
            for c in range(NC):
                for j in range(TOPK):
                    n = rows_of(c)
                    pool.indirect_dma_start(
                        out=picked[0:n, c * TOPK + j, :], out_offset=None, in_=rows,
                        in_offset=bass.IndirectOffsetOnAxis(ap=slot[0:n, c, j:j + 1], axis=0)
                    ).then_inc(picked_in[c], 16)

        @block.scalar
        def _(act):
            def first_rows(c):
                n = rows_of(c)
                act.wait_ge(tok_done, c + 1)
                act.activation(h[0:n, c, :], ps[0:n, c, 0:D], ACT.Copy).then_inc(h_ready, 1)

            def first_T(c):
                n = rows_of(c)
                act.wait_ge(xnT_done, c + 1)
                act.activation(xnT[:, :, c * P:c * P + n],
                               ps[:, 5 + c % 2, 0:KD * n].rearrange("p (k n) -> p k n", k=KD),
                               ACT.Copy).then_inc(xnT_ready, 1)

            def queries(j):
                for m in range(2):
                    act.wait_ge(q_done, 2 * j + m + 1)
                    act.activation(qT[:, BH * j:BH * j + BH, m, :],
                                   ps[:, (1, 4)[j] + m, 0:HALF].rearrange("p (b s) -> p b s", s=S),
                                   ACT.Copy).then_inc(q_ready, 1)

            first_rows(0)
            first_rows(1)
            first_rows(2)
            first_T(0)
            first_rows(3)
            first_T(1)
            first_rows(4)
            first_T(2)
            queries(0)
            first_T(3)
            first_T(4)
            queries(1)

            def exps(i):
                act.wait_ge(shifted, i + 1)
                act.activation(prob[:, i % 2, :, :, :], prob[:, i % 2, :, :, :], ACT.Exp,
                               scale=HD ** -0.5).then_inc(p_ready, 1)

            def probs_out(i):
                for b in range(IG):
                    act.wait_ge(pT_done, 2 * i + b + 1)
                    act.activation(probT[:, b, :], ps[0:MS, 4 + b, 0:4 * MS], ACT.Copy).then_inc(pT_ready, 1)

            def context_out(i):
                act.wait_ge(cT_done, i + 1)
                act.activation(
                    ctxT[:, :, i * IG * S:(i + 1) * IG * S].rearrange("p m (b s) -> p b m s", s=S),
                    ps[:, 6, 4 * 2 * G2:4 * 2 * G2 + IG * MS].rearrange("p (b m s) -> p b m s", b=IG, m=2),
                    ACT.Copy).then_inc(ctxT_ready, 1)

            def extra(i, at):
                for stage, c in EXTRA.get((i, at), ()):
                    n = rows_of(c)
                    bank = CHUNK_BANK[c]
                    if stage == "X":
                        act.wait_ge(xn2T_done, c + 1)
                        act.activation(xnT[:, :, c * P:c * P + n],
                                       ps[:, bank, D:D + KD * n].rearrange("p (k n) -> p k n", k=KD),
                                       ACT.Copy).then_inc(xn2T_ready, 1)
                    if stage == "R":
                        act.wait_ge(neg_ready, c + 1)
                        act.activation(ex[0:n, c, :], best[0:n, c, :], ACT.Exp, bias=neg_top[0:n, c:c + 1],
                                       accum_out=den[0:n, c:c + 1]).then_inc(ex_ready, 1)

            exps(0)
            exps(1)
            probs_out(0)
            for i in range(NG):
                extra(i, "a")
                if i + 1 < NG:
                    probs_out(i + 1)
                context_out(i)
                if i + 2 < NG:
                    exps(i + 2)
                extra(i, "b")

            def hidden(t):
                for q in range(FC // 2):
                    act.wait_ge(up_done, FC // 2 * t + q + 1)
                    act.activation(hidT[:, 2 * q:2 * q + 2, :],
                                   ps[:, UP + q, 0:2 * CAP].rearrange("p (k n) -> p k n", k=2),
                                   ACT.Gelu_apprx_tanh).then_inc(hid_ready, 1)

            with act.Fori(0, E) as t:
                hidden(t)
            with act.If(over(act)):
                with act.Fori(E, T_END) as t:
                    hidden(t)

        @block.vector
        def _(dve):
            steps = [0]

            def chain(ins):
                steps[0] += 1
                ins.then_inc(step, 1)
                dve.wait_ge(step, steps[0])

            dve.memset(ones_bf[:, :], 1.0).then_inc(const_ready, 1)

            def moments(c, ready):
                n = rows_of(c)
                chain(dve.bn_stats(stats[0:n, c, :], h[0:n, c, :]))
                dve.bn_aggr(mv[0:n, c, :], stats[0:n, c, :]).then_inc(ready, 1)

            def doubled(j):
                for i in range(2):
                    dve.tensor_copy(
                        twice[:, :, BH * j:BH * j + BH, i, :],
                        xnT[:, :, j * HALF:(j + 1) * HALF].rearrange("p k (b s) -> p k b s", s=S)
                    ).then_inc(twice_ready, 1)

            def keys(j):
                dve.wait_ge(k_done, j + 1)
                for g in range(NKV):
                    dve.tensor_scalar(kbd[:, BH * j:BH * j + BH, g, :],
                                      ps[:, 3 * j, 0:HALF].rearrange("p (b t) -> p b t", t=S),
                                      cst[:, C_GMASK + g:C_GMASK + g + 1], None, ALU.mult).then_inc(k_ready, 1)

            vmask = cst[0:MS, C_VMASK:C_VMASK + 2].unsqueeze(1)

            def values(j):
                dve.wait_ge(v_done, j + 1)
                dve.tensor_tensor(
                    vbd[:, B * j:B * j + B, :, 0:HD],
                    ps[0:MS, 7 - j, :].rearrange("p (b g d) -> p b g d", g=2, d=HD),
                    vmask.unsqueeze(3).to_broadcast([MS, B, 2, HD]), ALU.mult).then_inc(v_ready, 1)

            for c in range(NC):
                dve.wait_ge(h_ready, c + 1)
                moments(c, stats_ready)
                if c == 1:
                    dve.wait_ge(const_in, 16)
                    dve.tensor_copy(amask[:, :], cst[:, C_AMASK:C_AMASK + GT]).then_inc(const_ready, 1)
                    dve.tensor_copy(ident_bf[:, :], ident).then_inc(const_ready, 1)
                    dve.tensor_copy(upper_bf[:, :], cst[:, C_UPPER:C_UPPER + P]).then_inc(const_ready, 1)
                    dve.tensor_copy(vbd[:, :, :, HD],
                                    vmask.to_broadcast([MS, 2 * B, 2])).then_inc(v_ready, 1)
            dve.wait_ge(xnT_ready, 3)
            doubled(0)
            keys(0)
            values(0)
            dve.wait_ge(xnT_ready, NC)
            doubled(1)
            keys(1)
            values(1)

            def shift(i):
                par = i % 2
                sc = ps[0:MS, 2 * par:2 * par + 2, 0:IG * GT].rearrange("p m (g t) -> p m g t", t=S)
                dve.wait_ge(s_done, 2 * (i + 1))
                dve.tensor_reduce(top[:, par, :, :], sc, AX.X, ALU.max).then_inc(top_ready, 1)
                dve.wait_ge(top_ready, i + 1)
                if i >= 2:
                    dve.wait_ge(pT_done, 2 * (i - 1))
                dve.tensor_tensor(prob[:, par, :, :, :], sc,
                                  top[:, par, :, :].unsqueeze(3).to_broadcast([MS, 2, IG * NKV, S]),
                                  ALU.subtract).then_inc(shifted, 1)

            def context(i):
                dve.wait_ge(c_done, i + 1)
                acc = ps[0:MS, 6, 0:IG * 4 * G2].rearrange("p (r d) -> p r d", d=HD + 1)
                dve.reciprocal(rsum[:, :], acc[:, :, HD]).then_inc(rsum_ready, 1)
                dve.wait_ge(rsum_ready, i + 1)
                dve.tensor_tensor(ctxn[:, :, :].rearrange("p b (r d) -> p (b r) d", d=HD), acc[:, :, 0:HD],
                                  rsum[:, :].unsqueeze(2).to_broadcast([MS, 4 * NKV, HD]),
                                  ALU.mult).then_inc(ctxn_ready, 1)

            def extra(i, at):
                for stage, c in EXTRA.get((i, at), ()):
                    n = rows_of(c)
                    bank = CHUNK_BANK[c]
                    if stage == "W":
                        dve.wait_ge(wo_done, c + 1)
                        chain(dve.tensor_tensor(h[0:n, c, :], h[0:n, c, :], ps[0:n, bank, 0:D], ALU.add))
                        moments(c, stats2_ready)
                    if stage == "R":
                        dve.wait_ge(logits_done, c + 1)
                        chain(dve.tensor_copy(lg[0:n, c, :], ps[0:n, bank, 0:E]))
                        chain(dve.max(best[0:n, c, :], lg[0:n, c, :]))
                        dve.tensor_scalar(neg_top[0:n, c:c + 1], best[0:n, c, 0:1], -1.0, None,
                                          ALU.mult).then_inc(neg_ready, 1)
                        chain(dve.max_index(best_at[0:n, c, :], best[0:n, c, :], lg[0:n, c, :]))
                        chain(dve.tensor_tensor(
                            mask[0:n, c, :, :],
                            cst[0:n, C_EXPERT:C_EXPERT + E].unsqueeze(1).to_broadcast([n, TOPK, E]),
                            best_at[0:n, c, 0:TOPK].unsqueeze(2).to_broadcast([n, TOPK, E]), ALU.is_equal))
                        dve.tensor_tensor(both[0:n, c, :], mask[0:n, c, 0, :], mask[0:n, c, 1, :],
                                          ALU.add).then_inc(both_ready, 1)
                    if stage == "K":
                        dve.wait_ge(rank_done, c + 1)
                        dve.tensor_tensor(place[0:n, c, :], ps[0:n, bank, 16:16 + E],
                                          cst[0:n, C_BASE:C_BASE + E], ALU.add).then_inc(place_ready, 1)
                        dve.wait_ge(place_ready, c + 1)
                        chain(dve.tensor_tensor(
                            place_k[0:n, c, :, :], mask[0:n, c, :, :],
                            place[0:n, c, :].unsqueeze(1).to_broadcast([n, TOPK, E]), ALU.mult))
                        chain(dve.tensor_reduce(slot_f[0:n, c, :], place_k[0:n, c, :, :], AX.X, ALU.add))
                        dve.tensor_copy(slot[0:n, c, :], slot_f[0:n, c, :]).then_inc(slots_ready, 1)

            shift(0)
            shift(1)
            for i in range(NG):
                context(i)
                extra(i, "a")
                if i + 2 < NG:
                    shift(i + 2)
                extra(i, "b")

            count = ps[0:1, CHUNK_BANK[NC - 1], 32:32 + E]
            chain(dve.tensor_tensor(
                beyond[:, :, :], count.unsqueeze(2).to_broadcast([1, E, BLOCKS - 1]),
                cst[0:1, C_LIMIT:C_LIMIT + BLOCKS - 1].unsqueeze(1).to_broadcast([1, E, BLOCKS - 1]), ALU.is_gt))
            chain(dve.tensor_reduce(used[:, :], beyond[:, :, :], AX.X, ALU.add))
            chain(dve.tensor_tensor_scan(end[:, :], used[:, :], used[:, :], 0.0, ALU.add, ALU.max))
            j_of = cst[0:1, C_TILE:C_TILE + OVER]
            ends = end[:, :].unsqueeze(1).to_broadcast([1, OVER, E])
            chain(dve.tensor_tensor(ended[:, :, :], ends, j_of.unsqueeze(2).to_broadcast([1, OVER, E]), ALU.is_le))
            chain(dve.tensor_reduce(o_expert[:, :], ended[:, :, :], AX.X, ALU.add))
            chain(dve.tensor_tensor(begun[:, :, :], ended[:, :, :], ends, ALU.mult))
            chain(dve.tensor_reduce(o_block[:, :], begun[:, :, :], AX.X, ALU.max))
            chain(dve.tensor_tensor(o_block[:, :], j_of, o_block[:, :], ALU.subtract))
            chain(dve.tensor_scalar(o_block[:, :], o_block[:, :], 1.0, float(CAP), ALU.add, ALU.mult))
            chain(dve.scalar_tensor_tensor(o_row[:, :], o_expert[:, :], float(EROWS), o_block[:, :],
                                           ALU.mult, ALU.add))
            dve.tensor_scalar(over_tab[:, 0, :], o_expert[:, :], float(E - 1), None, ALU.min)
            chain(dve.tensor_copy(over_tab[:, 1, :], o_row[:, :]))
            dve.tensor_copy(over_any[:, :], end[:, E - 1:E]).then_inc(over_ready, 1)
            dve.wait_ge(ex_ready, NC)
            for c in range(NC):
                n = rows_of(c)
                chain(dve.reciprocal(den[0:n, c:c + 1], den[0:n, c:c + 1]))
                chain(dve.tensor_scalar(gate[0:n, c, :], ex[0:n, c, 0:TOPK], den[0:n, c:c + 1], None, ALU.mult))

            def rows_T(t):
                dve.wait_ge(xT_done, t + 1)
                dve.tensor_copy(x_T[:, :, :],
                                ps[:, XT, 0:KD * CAP].rearrange("p (k n) -> p k n", k=KD)).then_inc(xT_ready, 1)

            def result(t):
                dve.wait_ge(down_done, t + 1)
                dve.tensor_copy(yT[:, :, :], ps[:, DOWN:DOWN + KD, 0:CAP]).then_inc(yT_ready, 1)
                dve.wait_ge(yo_done, t + 1)
                if not (isinstance(t, int) and t == 0):
                    dve.wait_ge(y_out, 16 * t)
                dve.tensor_copy(y_sb[:, :, :],
                                ps[0:CR, YO, :].rearrange("p (r d) -> p r d", r=2)).then_inc(y_ready, 1)

            rows_T(0)
            rows_T(1)
            result(0)
            with dve.Fori(1, E - 1) as t:
                rows_T(t + 1)
                result(t)
            result(E - 1)
            with dve.If(over(dve)):
                rows_T(E)
                with dve.Fori(E, T_END - 1) as t:
                    rows_T(t + 1)
                    result(t)
                result(T_END - 1)

            for c in range(NC):
                n = rows_of(c)
                dve.wait_ge(picked_in[c], 16 * TOPK)
                chain(dve.scalar_tensor_tensor(h[0:n, c, :], picked[0:n, c * TOPK, :], gate[0:n, c, 0:1],
                                               h[0:n, c, :], ALU.mult, ALU.add))
                dve.scalar_tensor_tensor(h[0:n, c, :], picked[0:n, c * TOPK + 1, :], gate[0:n, c, 1:2],
                                         h[0:n, c, :], ALU.mult, ALU.add).then_inc(out_ready, 1)

        @block.tensor
        def _(pe):
            def embed(c, k):
                n = rows_of(c)
                mm = pe.matmul(ps[0:n, c, 0:D], patches_sb[:, k, c * P:c * P + n], w_tok_sb[:, k, :],
                               start=False, stop=(k == KP - 1))
                if k == KP - 1:
                    mm.then_inc(tok_done, 1)

            def first_T(c):
                n = rows_of(c)
                pe.wait_ge(xn_ready, c + 1)
                if c >= 2:
                    pe.wait_ge(xnT_ready, c - 1)
                for k in range(KD):
                    mm = pe.transpose(ps[:, 5 + c % 2, k * n:(k + 1) * n], xn[0:n, c, k * P:(k + 1) * P],
                                      ident[0:n, 0:n])
                mm.then_inc(xnT_done, 1)

            pe.wait_ge(pos_in, 64)
            for c in range(NC):
                n = rows_of(c)
                pe.matmul(ps[0:n, c, 0:D], pos_rows_sb[:, c * P:c * P + n], pos_sb[:, :], start=True, stop=False)
            for k in range(KP):
                if k % 2 == 0:
                    pe.wait_ge(patch_in[k // 2], 32)
                for c in range(2):
                    embed(c, k)
            for k in range(KP):
                embed(2, k)
            pe.wait_ge(const_in, 16)
            for c in range(3, NC):
                first_T(c - 3)
                for k in range(KP):
                    embed(c, k)
            first_T(2)

            def project(j):
                for k in range(KD):
                    mm = pe.matmul(ps[:, 3 * j, 0:HALF], wk_sb[:, k, :, :].rearrange("p i f -> p (i f)"),
                                   xnT[:, k, j * HALF:(j + 1) * HALF], start=(k == 0), stop=(k == KD - 1))
                mm.then_inc(k_done, 1)
                for m in range(2):
                    for k in range(KD):
                        mm = pe.matmul(ps[:, (1, 4)[j] + m, 0:HALF], wq_sb[:, k, m, :],
                                       xnT[:, k, j * HALF:(j + 1) * HALF], start=(k == 0), stop=(k == KD - 1))
                    mm.then_inc(q_done, 1)

            def values(j):
                pe.wait_ge(twice_ready, 2 * (j + 1))
                for b in range(BH):
                    for k in range(KD):
                        mm = pe.matmul(ps[0:MS, 7 - j, b * NKV * HD:(b + 1) * NKV * HD],
                                       twice[:, k, BH * j + b, :, :].rearrange("p i s -> p (i s)"),
                                       wv_sb[:, k, :], start=(k == 0), stop=(k == KD - 1))
                mm.then_inc(v_done, 1)

            pe.wait_ge(attn_in, 96)
            pe.wait_ge(xnT_ready, 3)
            pe.wait_ge(h_ready, 3)
            project(0)
            first_T(3)
            values(0)
            first_T(4)
            pe.wait_ge(xnT_ready, NC)
            pe.wait_ge(h_ready, NC)
            project(1)
            values(1)

            def scores(i, m):
                for b in range(IG):
                    dst = ps[0:MS, 2 * (i % 2) + m, b * GT:(b + 1) * GT]
                    pe.matmul(dst, ident_bf[0:MS, 0:MS], amask[0:MS, :], start=True, stop=False)
                    mm = pe.matmul(
                        dst, qT[m * 64:m * 64 + 64, IG * i + b, :, :].rearrange("p m s -> p (m s)"),
                        kbd[m * 64:m * 64 + 64, IG * i + b, :, :].rearrange("p g t -> p (g t)"),
                        start=False, stop=True)
                mm.then_inc(s_done, 1)

            def probs_T(i):
                pe.wait_ge(p_ready, i + 1)
                if i >= 1:
                    pe.wait_ge(pT_ready, 2 * i)
                for b in range(IG):
                    for m in range(2):
                        for g in range(2):
                            n = (2 * m + g) * MS
                            src = prob[:, i % 2, m, b * NKV + 2 * g:b * NKV + 2 * g + 2, :]
                            mm = pe.transpose(ps[0:MS, 4 + b, n:n + MS], src.rearrange("p g t -> p (g t)"),
                                              ident[0:MS, 0:MS])
                    mm.then_inc(pT_done, 1)

            def context(i):
                if i >= 1:
                    pe.wait_ge(ctxT_ready, i)
                for b in range(IG):
                    pe.wait_ge(pT_ready, 2 * i + b + 1)
                    for m in range(2):
                        for g in range(2):
                            r = (b * 2 + m) * 2 + g
                            mm = pe.matmul(ps[0:MS, 6, r * G2:(r + 1) * G2],
                                           probT[:, b, (2 * m + g) * MS:(2 * m + g + 1) * MS],
                                           vbd[:, (IG * i + b) * 2 + g, :, :].rearrange("p g d -> p (g d)"),
                                           start=True, stop=True)
                mm.then_inc(c_done, 1)

            def context_T(i):
                pe.wait_ge(ctxn_ready, i + 1)
                for b in range(IG):
                    at = 4 * 2 * G2 + b * MS
                    mm = pe.transpose(ps[:, 6, at:at + MS], ctxn[:, b, :], ident[0:MS, 0:MS])
                mm.then_inc(cT_done, 1)

            def extra(i, at):
                for stage, c in EXTRA.get((i, at), ()):
                    n = rows_of(c)
                    bank = CHUNK_BANK[c]
                    if stage == "W":
                        pe.wait_ge(ctxT_ready, images_of(c))
                        if c in (1, 4):
                            pe.wait_ge(place_ready, {1: 1, 4: 2}[c])
                        for m in range(2):
                            mm = pe.matmul(ps[0:n, bank, 0:D], ctxT[:, m, c * P:c * P + n], wo_sb[:, m, :],
                                           start=(m == 0), stop=(m == 1))
                        mm.then_inc(wo_done, 1)
                    if stage == "X":
                        pe.wait_ge(xn2_ready, c + 1)
                        for k in range(KD):
                            mm = pe.transpose(ps[:, bank, D + k * n:D + (k + 1) * n],
                                              xn[0:n, c, k * P:(k + 1) * P], ident[0:n, 0:n])
                        mm.then_inc(xn2T_done, 1)
                    if stage == "R":
                        pe.wait_ge(xn2T_ready, c + 1)
                        for k in range(KD):
                            mm = pe.matmul(ps[0:n, bank, 0:E], xnT[:, k, c * P:c * P + n], wr_sb[:, k, :],
                                           start=(k == 0), stop=(k == KD - 1))
                        mm.then_inc(logits_done, 1)
                    if stage == "K":
                        pe.wait_ge(both_ready, c + 1)
                        for d in range(c):
                            pe.matmul(ps[0:n, bank, 16:16 + E], ones_bf[0:P, 0:n], both[:, d, :],
                                      start=(d == 0), stop=False)
                        mm = pe.matmul(ps[0:n, bank, 16:16 + E], upper_bf[0:n, 0:n], both[0:n, c, :],
                                       start=(c == 0), stop=True)
                        if c == NC - 1:
                            for d in range(NC):
                                r = rows_of(d)
                                mm = pe.matmul(ps[0:n, bank, 32:32 + E], ones_bf[0:r, 0:n], both[0:r, d, :],
                                               start=(d == 0), stop=(d == NC - 1))
                        mm.then_inc(rank_done, 1)

            pe.wait_ge(const_ready, 4)
            pe.wait_ge(q_ready, 4)
            pe.wait_ge(k_ready, 2 * NKV)
            pe.wait_ge(v_ready, 3)
            for i in range(2):
                for m in range(2):
                    scores(i, m)
            probs_T(0)
            for i in range(NG):
                more = i + 2 < NG
                if more:
                    pe.wait_ge(shifted, i + 1)
                    scores(i + 2, 0)
                context(i)
                if i == NG - 2:
                    pe.wait_ge(shifted, NG)
                extra(i, "a")
                if more:
                    scores(i + 2, 1)
                if i + 1 < NG:
                    probs_T(i + 1)
                context_T(i)
                extra(i, "b")

            def rows_T(t):
                pe.wait_ge(x_in, 16 * (t + 1))
                if not (isinstance(t, int) and t == 0):
                    pe.wait_ge(xT_ready, t)
                for k in range(KD):
                    for r in range(2):
                        at = k * CAP + r * CR
                        mm = pe.transpose(ps[:, XT, at:at + CR], x_sb[:, r, k * P:(k + 1) * P],
                                          ident[0:CR, 0:CR])
                mm.then_inc(xT_done, 1)

            def up(t, i, parts):
                for q in parts:
                    if not (isinstance(t, int) and t == 0):
                        pe.wait_ge(hid_ready, FC // 2 * (t - 1) + q + 1)
                    for f in (2 * q, 2 * q + 1):
                        for k in range(KD):
                            mm = pe.matmul(ps[:, UP + q, (f % 2) * CAP:(f % 2 + 1) * CAP],
                                           wi_sb[:, i, k, f::FC], x_T[:, k, :],
                                           start=(k == 0), stop=(k == KD - 1))
                    mm.then_inc(up_done, 1)

            def down(t, i, parts):
                for f in parts:
                    if f % 2 == 0:
                        pe.wait_ge(hid_ready, FC // 2 * t + f // 2 + 1)
                    for k in range(KD):
                        mm = pe.matmul(ps[:, DOWN + k, 0:CAP], w2_sb[:, i, f, k * P:(k + 1) * P],
                                       hidT[:, f, :], start=(f == 0), stop=(f == FC - 1))
                if f == FC - 1:
                    mm.then_inc(down_done, 1)

            def result_T(t):
                pe.wait_ge(yT_ready, t + 1)
                if not (isinstance(t, int) and t == 0):
                    pe.wait_ge(y_ready, t)
                for r in range(2):
                    for k in range(KD):
                        at = r * D + k * P
                        mm = pe.transpose(ps[0:CR, YO, at:at + P], yT[:, k, r * CR:(r + 1) * CR], ident)
                mm.then_inc(yo_done, 1)

            def start(t, i, k):
                rows_T(t)
                pe.wait_ge(wi_in[i], 16 * (k + 1))
                pe.wait_ge(xT_ready, t + 1)
                up(t, i, range(FC // 2))

            def tile(t, i, k, k_next):
                pe.wait_ge(w2_in[i], 16 * (k + 1))
                down(t, i, range(FC // 2))
                rows_T(t + 1)
                down(t, i, range(FC // 2, FC))
                pe.wait_ge(wi_in[1 - i], 16 * (k_next + 1))
                pe.wait_ge(xT_ready, t + 2)
                up(t + 1, 1 - i, range(1))
                result_T(t)
                up(t + 1, 1 - i, range(1, FC // 2))

            def finish(t, i, k):
                pe.wait_ge(w2_in[i], 16 * (k + 1))
                down(t, i, range(FC))
                result_T(t)

            def tiles(first, last, loop_from):
                for t in range(first, 2 * loop_from):
                    tile(t, t % 2, t // 2, (t + 1) // 2)
                with pe.Fori(loop_from, last // 2) as k:
                    tile(2 * k, 0, k, k)
                    tile(2 * k + 1, 1, k, k + 1)
                tile(last - 1, 0, (last - 1) // 2, last // 2)
                finish(last, 1, last // 2)

            start(0, 0, 0)
            tiles(0, E - 1, 1)
            with pe.If(over(pe)):
                start(E, 0, E // 2)
                tiles(E, T_END - 1, E // 2)


def kernel(x, L0_tok_W, L0_tok_b, L0_tok_cls_token, L0_tok_pos_embedding, L0_attn_wq, L0_attn_wk, L0_attn_wv,
           L0_attn_wo, L0_ffn_w_router, L0_ffn_wi, L0_ffn_wo):
    import concourse.bacc as bacc
    from concourse.bass_utils import run_bass_kernel_spmd

    x, w, wq, wk, wv, wo = (np.asarray(a) for a in (x, L0_tok_W, L0_attn_wq, L0_attn_wk, L0_attn_wv, L0_attn_wo))
    patches = np.zeros((C * PATCH * PATCH, N), x.dtype)
    patches.reshape(-1, B, S)[:, :, 1:] = \
        x.reshape(B, C, GRID, PATCH, GRID, PATCH).transpose(1, 3, 5, 0, 2, 4).reshape(-1, B, S - 1)

    def by_partition(a):
        return np.ascontiguousarray(a.reshape(a.shape[0] // P, P, -1).transpose(1, 0, 2))

    q = wq.T.reshape(D, NKV, 2, 2, HD).transpose(0, 3, 2, 1, 4).reshape(KD, P, 2, P).transpose(1, 0, 2, 3)
    o = wo.T.reshape(NKV, 2, 2, HD, D).transpose(2, 1, 0, 3, 4).reshape(2, P, D).transpose(1, 0, 2)
    arrays = {
        "patches": by_partition(patches), "w_tok": by_partition(w.T), "bias": np.asarray(L0_tok_b),
        "cls": np.asarray(L0_tok_cls_token), "pos": np.asarray(L0_tok_pos_embedding),
        "wq": np.ascontiguousarray(q), "wk": by_partition(wk.T), "wv": by_partition(wv.T),
        "wo": np.ascontiguousarray(o), "w_router": np.asarray(L0_ffn_w_router),
        "wi": np.asarray(L0_ffn_wi), "w2": np.asarray(L0_ffn_wo),
        "consts": constants(), "pos_rows": position_rows(),
    }
    nc = bacc.Bacc("TRN2", target_bir_lowering=False, num_devices=1)
    args = [nc.dram_tensor(f"in_{n}", a.shape, mybir.dt.from_np(a.dtype), kind="ExternalInput").ap()
            for n, a in arrays.items()]
    out = nc.dram_tensor("out", (N, D), F32, kind="ExternalOutput").ap()
    vit_block(nc, *args, out)
    r = run_bass_kernel_spmd(nc, [{f"in_{n}": a for n, a in arrays.items()}], core_ids=[0])
    return r.results[0]["out"].reshape(B, S, D)
```

```python
from contextlib import ExitStack

import numpy as np

import concourse.bass as bass
from concourse import mybir

F32 = mybir.dt.float32
BF16 = mybir.dt.bfloat16
I32 = mybir.dt.int32
U32 = mybir.dt.uint32
ALU = mybir.AluOpType
ACT = mybir.ActivationFunctionType
AX = mybir.AxisListType

P = 128
B, C, IMG, PATCH, D = 16, 3, 96, 16, 256
GRID = IMG // PATCH
S = GRID * GRID + 1
SP = S + 2
N = B * S
NC = -(-N // P)
LAST = N - (NC - 1) * P
KP = C * PATCH * PATCH // P
KD = D // P
NKV, GS, HD = 4, 4, 16
GT = NKV * S
MS = 2 * S
GV = NKV * (HD + 1)
IG = 2
NG = B // IG
BH = B // 2
HALF = N // 2
E, F, TOPK = 8, 1024, 2
FC = F // P
CAP = 224
CR = CAP // 2
WIDTHS = (128, 152, 192, CAP)
BLOCKS = -(-N // CAP)
EROWS = -(-BLOCKS * CAP // 64) * 64
EPS = 1e-5
NEG = -1e30


def most_tiles_over():
    best = np.zeros(N * TOPK + 1, int)
    for _ in range(E):
        nxt = best.copy()
        for extra in range(1, BLOCKS):
            need = CAP * extra + 1
            nxt[need:] = np.maximum(nxt[need:], best[:-need] + extra)
        best = nxt
    return int(best[-1])


OVER = most_tiles_over()
OVER += OVER % 2
T_END = E + OVER
ROWS = E * EROWS + (OVER + 1) * CAP
DW = D + 16

EXTRA = {
    (2, "a"): [("W", 0), ("M", 0)],
    (3, "a"): [("X", 0)],
    (3, "b"): [("R", 0)],
    (4, "a"): [("K", 0)],
    (4, "b"): [("W", 1), ("M", 1)],
    (5, "a"): [("X", 1)],
    (5, "b"): [("R", 1)],
    (6, "a"): [("K", 1), ("W", 2), ("M", 2)],
    (6, "b"): [("X", 2)],
    (7, "a"): [("W", 3)],
    (7, "b"): [("R", 2), ("W", 4), ("X", 3), ("M", 3), ("X", 4), ("K", 2), ("M", 4), ("R", 3), ("R", 4),
               ("K", 3), ("K", 4)],
}
CHUNK_BANK = [7, 7, 0, 1, 7]

C_IDENT = 0
C_AMASK = C_IDENT + P
C_GMASK = C_AMASK + GT
C_VMASK = C_GMASK + NKV
C_UPPER = C_VMASK + 2 * NKV
C_EXPERT = C_UPPER + P
C_BASE = C_EXPERT + E
C_LIMIT = C_BASE + E
C_TILE = C_LIMIT + BLOCKS - 1
C_WIDTH = C_TILE + OVER
C_END = C_WIDTH + len(WIDTHS) - 1


def constants():
    c = np.zeros((P, C_END), np.float32)
    p = np.arange(P)
    c[:, C_IDENT:C_IDENT + P] = np.eye(P)
    c[:, C_AMASK:C_AMASK + GT] = np.where(np.arange(GT)[None] % S > p[:, None] % S, NEG, 0.0)
    c[:, C_GMASK:C_GMASK + NKV] = (p[:, None] % (NKV * HD)) // HD == np.arange(NKV)[None]
    for pair in range(2):
        at = C_VMASK + pair * NKV
        c[:, at:at + NKV] = p[:, None] // S + 2 * pair == np.arange(NKV)[None]
    c[:, C_UPPER:C_UPPER + P] = p[:, None] < p[None]
    c[:, C_EXPERT:C_EXPERT + E] = np.arange(E)[None]
    c[:, C_BASE:C_BASE + E] = np.arange(E)[None] * EROWS
    c[:, C_LIMIT:C_LIMIT + BLOCKS - 1] = np.arange(1, BLOCKS)[None] * CAP
    c[:, C_TILE:C_TILE + OVER] = np.arange(OVER)[None]
    c[:, C_WIDTH:C_END] = WIDTHS[:-1]
    return c


def position_rows():
    n = np.arange(N)
    rows = np.zeros((3, SP, N + 2), np.float32)
    for s in range(S):
        rows[:, s, :N] = n % S == s
    rows[:, S, :N] = n % S != 0
    rows[:, S + 1, :N] = n % S == 0
    rows[1:, :, N] = -1
    rows[2:, :, N + 1] = -1
    return rows.reshape(3 * SP, N + 2)


def rows_of(c):
    return P if c < NC - 1 else LAST


def images_of(c):
    return -(-(c * P + rows_of(c)) // (IG * S))


def vit_block(nc, patches, w_tok, embeddings, wq, wk, wv, wo, w_router, wi, w2, consts, pos_rows, out):
    ctx = ExitStack()
    with ctx:
        def sb(name, shape, dt=F32):
            return ctx.enter_context(nc.sbuf_tensor(name, shape, dt))

        def sem(name):
            return ctx.enter_context(nc.semaphore(name))

        rows = nc.dram_tensor("rows", [ROWS, DW], F32, kind="Internal").ap()

        patches_sb = sb("patches_sb", [P, KP, N])
        w_tok_sb = sb("w_tok_sb", [P, KP, D])
        pos_rows_sb = sb("pos_rows_sb", [3 * SP, N + 2])
        pos_rows_bf = sb("pos_rows_bf", [3 * SP, N], BF16)
        pos_sb = sb("pos_sb", [3 * SP, D])
        pos_bf = sb("pos_bf", [3 * SP, D], BF16)
        pos_part = sb("pos_part", [3 * SP, D], BF16)
        cst = sb("cst", [P, C_END])
        wq_sb = sb("wq_sb", [P, KD, 2, P])
        wk_sb = sb("wk_sb", [P, KD, 2, NKV * HD])
        wv_sb = sb("wv_sb", [P, KD, NKV * HD])
        wo_sb = sb("wo_sb", [P, 2, D])
        wr_sb = sb("wr_sb", [P, KD, E])
        wr_mean = sb("wr_mean", [P, E])
        wr_c = sb("wr_c", [P, KD, E])
        amask = sb("amask", [P, GT], BF16)
        ident_bf = sb("ident_bf", [P, P], BF16)
        upper_bf = sb("upper_bf", [P, P], BF16)
        ones_bf = sb("ones_bf", [P, P], BF16)
        mean_of = sb("mean_of", [P, P])
        half = sb("half", [P, 1])
        spare = sb("spare", [CR, 2, DW])
        h = sb("h", [P, NC, D])
        xn = sb("xn", [P, NC, D])
        xr = sb("xr", [P, NC, TOPK, DW])
        xnT = sb("xnT", [P, KD, N])
        stats = sb("stats", [P, NC, 6])
        mv = sb("mv", [P, NC, 2])
        var = sb("var", [P, NC, 2])
        root = sb("root", [P, NC])
        newton = sb("newton", [P, NC])
        shift_n = sb("shift_n", [P, NC])
        rstd = sb("rstd", [P, NC])
        twice = sb("twice", [P, KD, B, 2, S])
        qT = sb("qT", [P, B, 2, S])
        kbd = sb("kbd", [P, B, NKV, S])
        vbd = sb("vbd", [MS, B, 2, NKV, HD + 1])
        top = sb("top", [MS, 2, 2, IG * NKV])
        prob = sb("prob", [MS, 2, 2, IG * NKV, S])
        probT = sb("probT", [MS, IG, 4 * MS])
        rsum = sb("rsum", [MS, 4 * NKV])
        ctxn = sb("ctxn", [MS, IG, 2 * NKV * HD])
        ctxT = sb("ctxT", [P, 2, N])
        best = sb("best", [P, NC, 8])
        best_at = sb("best_at", [P, NC, 8], U32)
        neg_top = sb("neg_top", [P, NC])
        ex = sb("ex", [P, NC, 8])
        den = sb("den", [P, NC])
        mask = sb("mask", [P, NC, TOPK, E])
        both = sb("both", [P, NC, E], BF16)
        base_bf = sb("base_bf", [1, E], BF16)
        place_k = sb("place_k", [P, NC, TOPK, E])
        slot_f = sb("slot_f", [P, NC, TOPK])
        slot = sb("slot", [P, NC, TOPK], I32)
        beyond = sb("beyond", [1, E, BLOCKS - 1])
        used = sb("used", [1, E])
        end = sb("end", [1, E])
        ended = sb("ended", [1, OVER, E])
        begun = sb("begun", [1, OVER, E])
        o_expert = sb("o_expert", [1, OVER])
        o_block = sb("o_block", [1, OVER])
        o_row = sb("o_row", [1, OVER])
        over_tab = sb("over_tab", [1, 2, OVER], I32)
        over_any = sb("over_any", [1, 1], I32)
        past = sb("past", [1, E, len(WIDTHS) - 1])
        past_sum = sb("past_sum", [1, E])
        width_of = sb("width_of", [1, E], I32)
        wi_sb = sb("wi_sb", [P, 2, KD, F])
        w2_sb = sb("w2_sb", [P, 2, FC, D])
        x_sb = sb("x_sb", [CR, 2, 2, DW])
        to = sb("to", [CR, 2, 2], I32)
        row_gate = sb("row_gate", [CR, 2])
        x_T = sb("x_T", [P, KD, CAP])
        hidT = sb("hidT", [P, FC, CAP])
        yT = sb("yT", [P, KD, CAP])
        y_sb = sb("y_sb", [CR, 2, D])

        ident = cst[:, C_IDENT:C_IDENT + P]

        ps = ctx.enter_context(nc.psum_tensor("ps", [P, 8, 512], F32))
        UP, DOWN, XT, YO = 0, 4, 6, 7

        pos_in = sem("pos_in")
        patch_in = [sem(f"patch_in{k}") for k in range(KP)]
        pos_ready = sem("pos_ready")
        const_in = sem("const_in")
        attn_in = sem("attn_in")
        wi_in = [sem(f"wi_in{i}") for i in range(2)]
        w2_in = [sem(f"w2_in{i}") for i in range(2)]
        cleared = sem("cleared")
        rows_ready = sem("rows_ready")
        const_ready = sem("const_ready")
        tok_done = sem("tok_done")
        h_ready = sem("h_ready")
        stats_ready = sem("stats_ready")
        root_ready = sem("root_ready")
        xn_ready = sem("xn_ready")
        xnT_done = sem("xnT_done")
        xnT_ready = sem("xnT_ready")
        twice_ready = sem("twice_ready")
        q_done = sem("q_done")
        q_ready = sem("q_ready")
        k_done = sem("k_done")
        k_ready = sem("k_ready")
        v_done = sem("v_done")
        v_ready = sem("v_ready")
        s_done = sem("s_done")
        top_ready = sem("top_ready")
        shifted = sem("shifted")
        p_ready = sem("p_ready")
        pT_done = sem("pT_done")
        pT_ready = sem("pT_ready")
        c_done = sem("c_done")
        rsum_ready = sem("rsum_ready")
        ctxn_ready = sem("ctxn_ready")
        cT_done = sem("cT_done")
        ctxT_ready = sem("ctxT_ready")
        wo_done = sem("wo_done")
        stats2_ready = sem("stats2_ready")
        root2_ready = sem("root2_ready")
        xn2_ready = sem("xn2_ready")
        h2_ready = sem("h2_ready")
        h2T_done = sem("h2T_done")
        h2T_ready = sem("h2T_ready")
        colsum_done = sem("colsum_done")
        logits_done = sem("logits_done")
        norm_ready = sem("norm_ready")
        neg_ready = sem("neg_ready")
        ex_ready = sem("ex_ready")
        both_ready = sem("both_ready")
        rank_done = sem("rank_done")
        place_ready = sem("place_ready")
        slots_ready = sem("slots_ready")
        over_ready = sem("over_ready")
        width_ready = sem("width_ready")
        over_cleared = sem("over_cleared")
        scattered = sem("scattered")
        x_in = [sem(f"x_in{i}") for i in range(2)]
        gates_ready = sem("gates_ready")
        to_ready = sem("to_ready")
        xT_done = sem("xT_done")
        xT_ready = sem("xT_ready")
        up_done = sem("up_done")
        hid_ready = sem("hid_ready")
        down_done = sem("down_done")
        yT_ready = sem("yT_ready")
        yo_done = sem("yo_done")
        y_ready = sem("y_ready")
        y_out = sem("y_out")
        gate_ready = sem("gate_ready")
        out_begun = sem("out_begun")
        step = sem("step")
        pool_step = sem("pool_step")

        block = ctx.enter_context(nc.Block())

        def over(eng):
            eng.wait_ge(over_ready, 1)
            return eng.value_load(over_any[0:1, 0:1], min_val=0, max_val=OVER) > 0

        @block.sync
        def _(sp):
            for k in range(KP):
                sp.dma_start(w_tok_sb[:, k, :], w_tok[:, k, :]).then_inc(patch_in[k], 16)
                sp.dma_start(patches_sb[:, k, :], patches[:, k, :]).then_inc(patch_in[k], 16)
                if k == KP // 2:
                    sp.dma_start(pos_sb[:, :], embeddings).then_inc(pos_in, 16)
                    sp.dma_start(pos_rows_sb[:, :], pos_rows).then_inc(pos_in, 16)
            sp.dma_start(cst[:, :], consts).then_inc(const_in, 16)
            for i in range(2):
                sp.dma_start(wk_sb[:, :, i, :], wk).then_inc(attn_in, 16)
            sp.dma_start(wq_sb[:, :, :, :], wq).then_inc(attn_in, 16)
            sp.dma_start(wv_sb[:, :, :], wv).then_inc(attn_in, 16)
            sp.dma_start(wo_sb[:, :, :], wo).then_inc(attn_in, 16)
            sp.dma_start(wr_sb[:, :, :], w_router.rearrange("(k p) e -> p k e", p=P)).then_inc(attn_in, 16)
            def clear(blocks, ready):
                sp.dma_start(blocks.rearrange("n (p r) d -> p n (r d)", r=2),
                             spare[:, :, :].rearrange("p r d -> p (r d)").unsqueeze(1)
                             .to_broadcast([CR, blocks.shape[0], 2 * DW])).then_inc(ready, 16)

            expert_rows = rows[0:E * EROWS, :].rearrange("(e m) d -> e m d", e=E)
            sp.wait_ge(cleared, 1)
            clear(expert_rows[:, 0:CAP, :], rows_ready)

            def load_wi(e, i):
                sp.dma_start(wi_sb[:, i, :, :],
                             wi[bass.ds(e, 1), :, :].rearrange("a (k p) f -> p (a k) f", p=P)
                             ).then_inc(wi_in[i], 16)

            def load_w2(e, i):
                sp.dma_start(w2_sb[:, i, :, :].rearrange("p k d -> p (k d)"),
                             w2[bass.ds(e, 1), :, :].rearrange("a (p k) d -> p (a k d)", p=P)
                             ).then_inc(w2_in[i], 16)

            def load_x(row, i):
                sp.dma_start(x_sb[:, i, :, :], rows[bass.ds(row, CAP), :].rearrange("(p r) d -> p r d", r=2)
                             ).then_inc(x_in[i], 16)

            def load_tile(t, i, row, e):
                sp.wait_ge(up_done, FC // 2 * (t - 1))
                load_wi(e, i)
                sp.wait_ge(xT_done, t - 1)
                sp.wait_ge(to_ready, t - 1)
                load_x(row, i)
                sp.wait_ge(down_done, t - 1)
                load_w2(e, i)

            for i in range(2):
                load_wi(i, i)
                load_w2(i, i)
            sp.dma_start(out[N:N + CAP, :].rearrange("(p r) d -> p r d", r=2), spare[:, :, 0:D]).then_inc(out_begun, 16)
            for c in range(NC):
                n = rows_of(c)
                sp.wait_ge(h2_ready, c + 1)
                sp.dma_start(out[c * P:c * P + n, :], h[0:n, c, :]).then_inc(out_begun, 16)
            sp.wait_ge(scattered, 16 * TOPK * NC)
            for i in range(2):
                load_x(i * EROWS, i)
            with sp.Fori(1, E // 2) as k:
                for i in range(2):
                    t = 2 * k + i
                    load_tile(t, i, t * EROWS, t)

            with sp.If(over(sp)):
                for j in range(1, BLOCKS):
                    clear(expert_rows[:, j * CAP:(j + 1) * CAP, :], over_cleared)
                clear(rows[E * EROWS:ROWS, :].rearrange("(n m) d -> n m d", m=CAP), over_cleared)
                sp.wait_ge(scattered, 2 * 16 * TOPK * NC)
                with sp.Fori(E // 2, T_END // 2) as k:
                    for i in range(2):
                        t = 2 * k + i
                        e = sp.value_load(over_tab[0:1, 0, bass.ds(t - E, 1)], min_val=0, max_val=E - 1)
                        row = sp.value_load(over_tab[0:1, 1, bass.ds(t - E, 1)], min_val=0, max_val=ROWS - CAP)
                        load_tile(t, i, row, e)
                sp.wait_ge(y_out, 32 * T_END)

            sp.wait_ge(y_out, 32 * E)

        @block.gpsimd
        def _(pool):
            steps = [0]

            def chain(ins):
                steps[0] += 1
                ins.then_inc(pool_step, 1)
                pool.wait_ge(pool_step, steps[0])

            chain(pool.memset(spare[:, :, :], 0.0))
            pool.iota(spare[:, :, D:D + 1].bitcast(I32), [[1, 2], [0, 1]], base=N,
                      channel_multiplier=2).then_inc(cleared, 1)
            chain(pool.memset(xr[:, :, :, D:DW], 0.0))
            pool.iota(xr[:, :, :, D:D + 1].bitcast(I32), [[P, NC], [0, TOPK], [0, 1]], base=0,
                      channel_multiplier=1).then_inc(rows_ready, 1)
            chain(pool.memset(half[:, :], -0.5))

            def root_of(c, wanted, ready):
                n = rows_of(c)
                pool.wait_ge(wanted, c + 1)
                pool.tensor_tensor(root[0:n, c:c + 1], var[0:n, c, 0:1], half[0:n, :], ALU.pow).then_inc(ready, 1)

            def scatter(c):
                n = rows_of(c)
                pool.wait_ge(xn2_ready, c + 1)
                pool.wait_ge(gate_ready, c + 1)
                pool.wait_ge(slots_ready, c + 1)
                for j in range(TOPK):
                    pool.indirect_dma_start(
                        out=rows, out_offset=bass.IndirectOffsetOnAxis(ap=slot[0:n, c, j:j + 1], axis=0),
                        in_=xr[0:n, c, j, :], in_offset=None).then_inc(scattered, 16)

            for c in range(NC):
                root_of(c, stats_ready, root_ready)
            root_of(0, stats2_ready, root2_ready)
            pool.wait_ge(rows_ready, 16 + 1)
            scatter(0)
            root_of(1, stats2_ready, root2_ready)
            scatter(1)
            root_of(2, stats2_ready, root2_ready)
            root_of(3, stats2_ready, root2_ready)
            root_of(4, stats2_ready, root2_ready)
            scatter(2)
            scatter(3)
            scatter(4)

            def results(t, i):
                pool.wait_ge(y_ready, t + 1)
                if not (isinstance(t, int) and t == 0):
                    pool.wait_ge(y_out, 32 * t)
                pool.nop(nofuse=True)
                for r in range(2):
                    pool.indirect_dma_start(
                        out=out, out_offset=bass.IndirectOffsetOnAxis(ap=to[:, i, r:r + 1], axis=0),
                        in_=y_sb[:, r, :], in_offset=None, compute_op=ALU.add).then_inc(y_out, 16)

            pool.wait_ge(out_begun, 16 * (NC + 1))
            results(0, 0)
            with pool.Fori(1, E // 2) as k:
                results(2 * k - 1, 1)
                results(2 * k, 0)
            results(E - 1, 1)
            with pool.If(over(pool)):
                pool.wait_ge(over_cleared, 16 * BLOCKS)
                for c in range(NC):
                    scatter(c)
                with pool.Fori(E // 2, T_END // 2) as k:
                    results(2 * k, 0)
                    results(2 * k + 1, 1)

        @block.scalar
        def _(act):
            def first_rows(c):
                n = rows_of(c)
                act.wait_ge(tok_done, c + 1)
                act.activation(h[0:n, c, :], ps[0:n, c, 0:D], ACT.Copy).then_inc(h_ready, 1)

            def first_T(c):
                n = rows_of(c)
                act.wait_ge(xnT_done, c + 1)
                act.activation(xnT[:, :, c * P:c * P + n],
                               ps[:, 5 + c % 2, 0:KD * n].rearrange("p (k n) -> p k n", k=KD),
                               ACT.Copy).then_inc(xnT_ready, 1)

            def keys(j):
                act.wait_ge(k_done, j + 1)
                for g in range(NKV):
                    act.activation(kbd[:, BH * j:BH * j + BH, g, :],
                                   ps[:, 3 * j, 0:HALF].rearrange("p (b t) -> p b t", t=S), ACT.Copy,
                                   scale=cst[:, C_GMASK + g:C_GMASK + g + 1]).then_inc(k_ready, 1)

            def queries(j):
                for m in range(2):
                    act.wait_ge(q_done, 2 * j + m + 1)
                    act.activation(qT[:, BH * j:BH * j + BH, m, :],
                                   ps[:, (1, 4)[j] + m, 0:HALF].rearrange("p (b s) -> p b s", s=S),
                                   ACT.Copy).then_inc(q_ready, 1)

            def exps(i):
                act.wait_ge(shifted, i + 1)
                act.activation(prob[:, i % 2, :, :, :], prob[:, i % 2, :, :, :], ACT.Exp,
                               scale=HD ** -0.5).then_inc(p_ready, 1)

            def probs_out(i):
                for b in range(IG):
                    act.wait_ge(pT_done, 2 * i + b + 1)
                    act.activation(probT[:, b, :], ps[0:MS, 4 + b, 0:4 * MS], ACT.Copy).then_inc(pT_ready, 1)

            def context_out(i):
                act.wait_ge(cT_done, i + 1)
                act.activation(
                    ctxT[:, :, i * IG * S:(i + 1) * IG * S].rearrange("p m (b s) -> p b m s", s=S),
                    ps[:, 6, IG * 2 * GV:IG * 2 * GV + IG * MS].rearrange("p (b m s) -> p b m s", b=IG, m=2),
                    ACT.Copy).then_inc(ctxT_ready, 1)

            def extra(i, at):
                for stage, c in EXTRA.get((i, at), ()):
                    n = rows_of(c)
                    bank = CHUNK_BANK[c]
                    if stage == "X":
                        act.wait_ge(h2T_done, c + 1)
                        act.activation(xnT[:, :, c * P:c * P + n],
                                       ps[:, bank, D:D + KD * n].rearrange("p (k n) -> p k n", k=KD),
                                       ACT.Copy).then_inc(h2T_ready, 1)
                    if stage == "R":
                        act.wait_ge(neg_ready, c + 1)
                        act.activation(ex[0:n, c, :], best[0:n, c, :], ACT.Exp, bias=neg_top[0:n, c:c + 1],
                                       scale=rstd[0:n, c:c + 1], accum_out=den[0:n, c:c + 1]).then_inc(ex_ready, 1)
                        act.wait_ge(norm_ready, c + 1)
                        act.activation(xr[0:n, c, :, 0:D], h[0:n, c, :].unsqueeze(1).to_broadcast([n, TOPK, D]),
                                       ACT.Identity, bias=shift_n[0:n, c:c + 1],
                                       scale=rstd[0:n, c:c + 1]).then_inc(xn2_ready, 1)

            first_rows(0)
            first_rows(1)
            first_rows(2)
            first_rows(3)
            first_T(0)
            first_T(1)
            first_T(2)
            first_rows(4)
            act.wait_ge(const_in, 16)
            keys(0)
            queries(0)
            first_T(3)
            first_T(4)
            exps(0)
            keys(1)
            queries(1)
            probs_out(0)
            exps(1)
            for i in range(NG):
                extra(i, "a")
                if i + 1 < NG:
                    probs_out(i + 1)
                context_out(i)
                if i + 2 < NG:
                    exps(i + 2)
                extra(i, "b")

            def hidden(t):
                for q in range(FC // 2):
                    act.wait_ge(up_done, FC // 2 * t + q + 1)
                    act.activation(hidT[:, 2 * q:2 * q + 2, :],
                                   ps[:, UP + q, 0:2 * CAP].rearrange("p (k n) -> p k n", k=2),
                                   ACT.Gelu_apprx_tanh).then_inc(hid_ready, 1)

            with act.Fori(0, E) as t:
                hidden(t)
            with act.If(over(act)):
                with act.Fori(E, T_END) as t:
                    hidden(t)

        @block.vector
        def _(dve):
            steps = [0]

            def chain(ins):
                dve.wait_ge(step, counted(ins))

            def counted(ins):
                steps[0] += 1
                ins.then_inc(step, 1)
                return steps[0]

            dve.memset(ps[:, UP:UP + FC // 2, HALF:2 * CAP], 0.0).then_inc(const_ready, 1)
            dve.memset(ones_bf[:, :], 1.0).then_inc(const_ready, 1)
            dve.memset(mean_of[:, :], 1.0 / D).then_inc(const_ready, 1)

            dve.wait_ge(pos_in, 32)
            chain(dve.tensor_copy(pos_part[:, :], pos_sb[:, :]))
            chain(dve.scalar_tensor_tensor(pos_sb[:, :], pos_part[:, :], pos_rows_sb[:, N:N + 1], pos_sb[:, :],
                                           ALU.mult, ALU.add))
            chain(dve.tensor_copy(pos_part[:, :], pos_sb[:, :]))
            dve.scalar_tensor_tensor(pos_bf[:, :], pos_part[:, :], pos_rows_sb[:, N + 1:N + 2], pos_sb[:, :],
                                     ALU.mult, ALU.add).then_inc(pos_ready, 1)
            dve.tensor_copy(pos_rows_bf[:, :], pos_rows_sb[:, 0:N]).then_inc(pos_ready, 1)

            var_at = {}

            def moments(c, ready):
                n = rows_of(c)
                chain(dve.bn_stats(stats[0:n, c, :], h[0:n, c, :]))
                chain(dve.bn_aggr(mv[0:n, c, :], stats[0:n, c, :]))
                dve.tensor_scalar(var[0:n, c, 0:1], mv[0:n, c, 1:2], EPS, None, ALU.add).then_inc(ready, 1)
                var_at[c] = counted(dve.tensor_scalar(var[0:n, c, 1:2], mv[0:n, c, 1:2], EPS, -0.5,
                                                      ALU.add, ALU.mult))

            def normalise(c, wanted, dst, src, ready):
                n = rows_of(c)
                r, w = root[0:n, c:c + 1], newton[0:n, c:c + 1]
                dve.wait_ge(wanted, c + 1)
                dve.wait_ge(step, steps[0])
                chain(dve.tensor_scalar(w, r, var[0:n, c, 1:2], r, ALU.mult, ALU.mult))
                chain(dve.tensor_scalar(rstd[0:n, c:c + 1], w, 1.5, r, ALU.add, ALU.mult))
                dve.tensor_scalar(dst, src, mv[0:n, c, 0:1], rstd[0:n, c:c + 1],
                                  ALU.subtract, ALU.mult).then_inc(ready, 1)

            def doubled(j):
                for i in range(2):
                    dve.tensor_copy(
                        twice[:, :, BH * j:BH * j + BH, i, :],
                        xnT[:, :, j * HALF:(j + 1) * HALF].rearrange("p k (b s) -> p k b s", s=S)
                    ).then_inc(twice_ready, 1)

            vmask = cst[0:MS, C_VMASK:C_VMASK + 2 * NKV].rearrange("p (q g) -> p q g", q=2)

            def values(j):
                dve.wait_ge(v_done, j + 1)
                for pair in range(2):
                    dve.tensor_tensor(
                        vbd[:, BH * j:BH * j + BH, pair, :, 0:HD],
                        ps[0:MS, 7 - j, :].rearrange("p (b g d) -> p b g d", g=NKV, d=HD),
                        vmask[:, pair, :].unsqueeze(1).unsqueeze(3).to_broadcast([MS, BH, NKV, HD]),
                        ALU.mult).then_inc(v_ready, 1)

            def first_norm(c):
                n = rows_of(c)
                normalise(c, root_ready, xn[0:n, c, :], h[0:n, c, :], xn_ready)

            for c in range(NC):
                if c == NC - 1:
                    dve.wait_ge(xnT_ready, 3)
                    doubled(0)
                dve.wait_ge(h_ready, c + 1)
                moments(c, stats_ready)
                if c == 1:
                    dve.wait_ge(const_in, 16)
                    dve.tensor_copy(amask[:, :], cst[:, C_AMASK:C_AMASK + GT]).then_inc(const_ready, 1)
                    dve.tensor_copy(ident_bf[:, :], ident).then_inc(const_ready, 1)
                    dve.tensor_copy(upper_bf[:, :], cst[:, C_UPPER:C_UPPER + P]).then_inc(const_ready, 1)
                    dve.tensor_copy(base_bf[:, :], cst[0:1, C_BASE:C_BASE + E]).then_inc(const_ready, 1)
                    dve.tensor_copy(vbd[:, :, :, :, HD],
                                    vmask.unsqueeze(1).to_broadcast([MS, B, 2, NKV])).then_inc(v_ready, 1)
                if c == 1:
                    first_norm(0)
                    first_norm(1)
                if c >= 2:
                    first_norm(c)
            def shift(i):
                par = i % 2
                sc = ps[0:MS, 2 * par:2 * par + 2, 0:IG * GT].rearrange("p m (g t) -> p m g t", t=S)
                dve.wait_ge(s_done, 2 * (i + 1))
                dve.tensor_reduce(top[:, par, :, :], sc, AX.X, ALU.max).then_inc(top_ready, 1)
                dve.wait_ge(top_ready, i + 1)
                if i >= 2:
                    dve.wait_ge(pT_done, 2 * (i - 1))
                dve.tensor_tensor(prob[:, par, :, :, :], sc,
                                  top[:, par, :, :].unsqueeze(3).to_broadcast([MS, 2, IG * NKV, S]),
                                  ALU.subtract).then_inc(shifted, 1)

            def context(i):
                dve.wait_ge(c_done, i + 1)
                acc = ps[0:MS, 6, 0:IG * 2 * GV].rearrange("p (r d) -> p r d", d=HD + 1)
                dve.reciprocal(rsum[:, :], acc[:, :, HD]).then_inc(rsum_ready, 1)
                dve.wait_ge(rsum_ready, i + 1)
                dve.tensor_tensor(ctxn[:, :, :].rearrange("p b (r d) -> p (b r) d", d=HD), acc[:, :, 0:HD],
                                  rsum[:, :].unsqueeze(2).to_broadcast([MS, 4 * NKV, HD]),
                                  ALU.mult).then_inc(ctxn_ready, 1)

            def extra(i, at):
                for stage, c in EXTRA.get((i, at), ()):
                    n = rows_of(c)
                    bank = CHUNK_BANK[c]
                    if stage == "W":
                        dve.wait_ge(wo_done, c + 1)
                        dve.tensor_tensor(h[0:n, c, :], h[0:n, c, :], ps[0:n, bank, 0:D],
                                          ALU.add).then_inc(h2_ready, 1)
                    if stage == "M":
                        dve.wait_ge(h2_ready, c + 1)
                        moments(c, stats2_ready)
                    if stage == "R":
                        col = slice(c, c + 1)
                        dve.wait_ge(logits_done, c + 1)
                        logits = ps[0:n, bank, 0:E]
                        found = counted(dve.max(best[0:n, c, :], logits))
                        dve.wait_ge(root2_ready, c + 1)
                        dve.wait_ge(step, var_at[c])
                        bent = counted(dve.tensor_scalar(newton[0:n, col], root[0:n, col], var[0:n, c, 1:2],
                                                         root[0:n, col], ALU.mult, ALU.mult))
                        dve.wait_ge(step, found)
                        placed = counted(dve.max_index(best_at[0:n, c, :], best[0:n, c, :], logits))
                        dve.wait_ge(step, bent)
                        scaled = counted(dve.tensor_scalar(rstd[0:n, col], newton[0:n, col], 1.5, root[0:n, col],
                                                           ALU.add, ALU.mult))
                        dve.wait_ge(step, placed)
                        masked = counted(dve.tensor_tensor(
                            mask[0:n, c, :, :],
                            cst[0:n, C_EXPERT:C_EXPERT + E].unsqueeze(1).to_broadcast([n, TOPK, E]),
                            best_at[0:n, c, 0:TOPK].unsqueeze(2).to_broadcast([n, TOPK, E]), ALU.is_equal))
                        dve.wait_ge(step, scaled)
                        dve.tensor_scalar(neg_top[0:n, col], best[0:n, c, 0:1], rstd[0:n, col], -1.0,
                                          ALU.mult, ALU.mult).then_inc(neg_ready, 1)
                        dve.wait_ge(step, masked)
                        dve.tensor_tensor(both[0:n, c, :], mask[0:n, c, 0, :], mask[0:n, c, 1, :],
                                          ALU.add).then_inc(both_ready, 1)
                        dve.tensor_scalar(shift_n[0:n, col], mv[0:n, c, 0:1], rstd[0:n, col], -1.0,
                                          ALU.mult, ALU.mult).then_inc(norm_ready, 1)
                    if stage == "K":
                        dve.wait_ge(rank_done, c + 1)
                        dve.tensor_tensor(
                            place_k[0:n, c, :, :], mask[0:n, c, :, :],
                            ps[0:n, bank, 16:16 + E].unsqueeze(1).to_broadcast([n, TOPK, E]),
                            ALU.mult).then_inc(place_ready, 1)
                        dve.wait_ge(ex_ready, c + 1)
                        turned = counted(dve.reciprocal(den[0:n, c:c + 1], den[0:n, c:c + 1]))
                        dve.wait_ge(place_ready, c + 1)
                        summed = counted(dve.tensor_reduce(slot_f[0:n, c, :], place_k[0:n, c, :, :], AX.X, ALU.add))
                        dve.wait_ge(step, turned)
                        dve.tensor_scalar(xr[0:n, c, :, D + 1], ex[0:n, c, 0:TOPK], den[0:n, c:c + 1], None,
                                          ALU.mult).then_inc(gate_ready, 1)
                        dve.wait_ge(step, summed)
                        dve.tensor_copy(slot[0:n, c, :], slot_f[0:n, c, :]).then_inc(slots_ready, 1)

            values(0)
            dve.wait_ge(xnT_ready, NC)
            doubled(1)
            shift(0)
            values(1)
            shift(1)
            dve.wait_ge(colsum_done, 1)
            chain(dve.tensor_copy(wr_mean[:, :], ps[:, 7, 0:E]))
            dve.tensor_tensor(wr_c[:, :, :], wr_sb[:, :, :], wr_mean[:, :].unsqueeze(1).to_broadcast([P, KD, E]),
                              ALU.subtract).then_inc(const_ready, 1)
            for i in range(NG):
                context(i)
                extra(i, "a")
                if i + 2 < NG:
                    shift(i + 2)
                extra(i, "b")

            count = ps[0:1, CHUNK_BANK[NC - 1], 32:32 + E]
            chain(dve.tensor_tensor(
                past[:, :, :], count.unsqueeze(2).to_broadcast([1, E, len(WIDTHS) - 1]),
                cst[0:1, C_WIDTH:C_END].unsqueeze(1).to_broadcast([1, E, len(WIDTHS) - 1]), ALU.is_gt))
            chain(dve.tensor_reduce(past_sum[:, :], past[:, :, :], AX.X, ALU.add))
            dve.tensor_copy(width_of[:, :], past_sum[:, :]).then_inc(width_ready, 1)

            chain(dve.tensor_tensor(
                beyond[:, :, :], count.unsqueeze(2).to_broadcast([1, E, BLOCKS - 1]),
                cst[0:1, C_LIMIT:C_LIMIT + BLOCKS - 1].unsqueeze(1).to_broadcast([1, E, BLOCKS - 1]), ALU.is_gt))
            chain(dve.tensor_reduce(used[:, :], beyond[:, :, :], AX.X, ALU.add))
            chain(dve.tensor_tensor_scan(end[:, :], used[:, :], used[:, :], 0.0, ALU.add, ALU.max))
            j_of = cst[0:1, C_TILE:C_TILE + OVER]
            ends = end[:, :].unsqueeze(1).to_broadcast([1, OVER, E])
            chain(dve.tensor_tensor(ended[:, :, :], ends, j_of.unsqueeze(2).to_broadcast([1, OVER, E]), ALU.is_le))
            chain(dve.tensor_reduce(o_expert[:, :], ended[:, :, :], AX.X, ALU.add))
            chain(dve.tensor_tensor(begun[:, :, :], ended[:, :, :], ends, ALU.mult))
            chain(dve.tensor_reduce(o_block[:, :], begun[:, :, :], AX.X, ALU.max))
            chain(dve.tensor_tensor(o_block[:, :], j_of, o_block[:, :], ALU.subtract))
            chain(dve.tensor_scalar(o_block[:, :], o_block[:, :], 1.0, float(CAP), ALU.add, ALU.mult))
            chain(dve.scalar_tensor_tensor(o_row[:, :], o_expert[:, :], float(EROWS), o_block[:, :],
                                           ALU.mult, ALU.add))
            dve.tensor_scalar(over_tab[:, 0, :], o_expert[:, :], float(E - 1), None, ALU.min)
            chain(dve.tensor_copy(over_tab[:, 1, :], o_row[:, :]))
            dve.tensor_copy(over_any[:, :], end[:, E - 1:E]).then_inc(over_ready, 1)

            def rows_T(t):
                dve.wait_ge(xT_done, t + 1)
                dve.tensor_copy(x_T[:, :, :],
                                ps[:, XT, 0:KD * CAP].rearrange("p (k n) -> p k n", k=KD)).then_inc(xT_ready, 1)

            def targets(t, i):
                if not (isinstance(t, int) and t < 2):
                    dve.wait_ge(y_out, 32 * (t - 1))
                if not (isinstance(t, int) and t == 0):
                    dve.wait_ge(y_ready, t)
                dve.tensor_copy(row_gate[:, :], x_sb[:, i, :, D + 1]).then_inc(gates_ready, 1)
                dve.tensor_copy(to[:, i, :], x_sb[:, i, :, D].bitcast(I32)).then_inc(to_ready, 1)

            def result(t):
                dve.wait_ge(down_done, t + 1)
                dve.tensor_copy(yT[:, :, :], ps[:, DOWN:DOWN + KD, 0:CAP]).then_inc(yT_ready, 1)
                dve.wait_ge(yo_done, t + 1)
                if not (isinstance(t, int) and t == 0):
                    dve.wait_ge(y_out, 32 * t)
                dve.wait_ge(gates_ready, t + 1)
                dve.tensor_tensor(y_sb[:, :, :], ps[0:CR, YO, :].rearrange("p (r d) -> p r d", r=2),
                                  row_gate[:, :].unsqueeze(2).to_broadcast([CR, 2, D]),
                                  ALU.mult).then_inc(y_ready, 1)

            def tile(t, i):
                rows_T(t + 1)
                targets(t, i)
                result(t)

            def last_tile(t):
                targets(t, 1)
                result(t)

            rows_T(0)
            tile(0, 0)
            tile(1, 1)
            with dve.Fori(1, E // 2 - 1) as k:
                tile(2 * k, 0)
                tile(2 * k + 1, 1)
            tile(E - 2, 0)
            last_tile(E - 1)
            with dve.If(over(dve)):
                rows_T(E)
                with dve.Fori(E // 2, T_END // 2 - 1) as k:
                    tile(2 * k, 0)
                    tile(2 * k + 1, 1)
                tile(T_END - 2, 0)
                last_tile(T_END - 1)

        @block.tensor
        def _(pe):
            def embed(c, k):
                n = rows_of(c)
                pe.matmul(ps[0:n, c, 0:D], patches_sb[:, k, c * P:c * P + n], w_tok_sb[:, k, :],
                          start=(k == 0), stop=False)
                if k == KP - 1:
                    pe.matmul(ps[0:n, c, 0:D], pos_rows_bf[:, c * P:c * P + n], pos_bf[:, :],
                              start=False, stop=True).then_inc(tok_done, 1)

            def first_T(c):
                n = rows_of(c)
                pe.wait_ge(xn_ready, c + 1)
                if c >= 2:
                    pe.wait_ge(xnT_ready, c - 1)
                for k in range(KD):
                    mm = pe.transpose(ps[:, 5 + c % 2, k * n:(k + 1) * n], xn[0:n, c, k * P:(k + 1) * P],
                                      ident[0:n, 0:n])
                mm.then_inc(xnT_done, 1)

            pe.wait_ge(const_ready, 1)
            for k in range(KP):
                pe.wait_ge(patch_in[k], 32)
                if k == KP - 1:
                    pe.wait_ge(pos_ready, 2)
                for c in range(2):
                    embed(c, k)
            for k in range(KP):
                embed(2, k)
            pe.wait_ge(const_in, 16)
            for k in range(KP):
                embed(3, k)
            first_T(0)
            first_T(1)
            for k in range(KP):
                embed(4, k)
                if k == KP // 2:
                    first_T(2)

            def project(j):
                for k in range(KD):
                    mm = pe.matmul(ps[:, 3 * j, 0:HALF], wk_sb[:, k, :, :].rearrange("p i f -> p (i f)"),
                                   xnT[:, k, j * HALF:(j + 1) * HALF], start=(k == 0), stop=(k == KD - 1))
                mm.then_inc(k_done, 1)
                for m in range(2):
                    for k in range(KD):
                        mm = pe.matmul(ps[:, (1, 4)[j] + m, 0:HALF], wq_sb[:, k, m, :],
                                       xnT[:, k, j * HALF:(j + 1) * HALF], start=(k == 0), stop=(k == KD - 1))
                    mm.then_inc(q_done, 1)

            def values(j):
                pe.wait_ge(twice_ready, 2 * (j + 1))
                for b in range(BH):
                    for k in range(KD):
                        mm = pe.matmul(ps[0:MS, 7 - j, b * NKV * HD:(b + 1) * NKV * HD],
                                       twice[:, k, BH * j + b, :, :].rearrange("p i s -> p (i s)"),
                                       wv_sb[:, k, :], start=(k == 0), stop=(k == KD - 1))
                mm.then_inc(v_done, 1)

            pe.wait_ge(attn_in, 96)
            pe.wait_ge(xnT_ready, 3)
            pe.wait_ge(h_ready, 3)
            def scores(i, m):
                for b in range(IG):
                    dst = ps[0:MS, 2 * (i % 2) + m, b * GT:(b + 1) * GT]
                    pe.matmul(dst, ident_bf[0:MS, 0:MS], amask[0:MS, :], start=True, stop=False)
                    mm = pe.matmul(
                        dst, qT[m * 64:m * 64 + 64, IG * i + b, :, :].rearrange("p m s -> p (m s)"),
                        kbd[m * 64:m * 64 + 64, IG * i + b, :, :].rearrange("p g t -> p (g t)"),
                        start=False, stop=True)
                mm.then_inc(s_done, 1)

            def probs_T(i):
                pe.wait_ge(p_ready, i + 1)
                if i >= 1:
                    pe.wait_ge(pT_ready, 2 * i)
                for b in range(IG):
                    for m in range(2):
                        for g in range(2):
                            n = (2 * m + g) * MS
                            src = prob[:, i % 2, m, b * NKV + 2 * g:b * NKV + 2 * g + 2, :]
                            mm = pe.transpose(ps[0:MS, 4 + b, n:n + MS], src.rearrange("p g t -> p (g t)"),
                                              ident[0:MS, 0:MS])
                    mm.then_inc(pT_done, 1)

            def context(i):
                if i >= 1:
                    pe.wait_ge(ctxT_ready, i)
                for b in range(IG):
                    pe.wait_ge(pT_ready, 2 * i + b + 1)
                    for m in range(2):
                        r = b * 2 + m
                        for g in range(2):
                            mm = pe.matmul(ps[0:MS, 6, r * GV:(r + 1) * GV],
                                           probT[:, b, (2 * m + g) * MS:(2 * m + g + 1) * MS],
                                           vbd[:, IG * i + b, g, :, :].rearrange("p g d -> p (g d)"),
                                           start=(g == 0), stop=(g == 1))
                mm.then_inc(c_done, 1)

            def context_T(i):
                pe.wait_ge(ctxn_ready, i + 1)
                for b in range(IG):
                    at = IG * 2 * GV + b * MS
                    mm = pe.transpose(ps[:, 6, at:at + MS], ctxn[:, b, :], ident[0:MS, 0:MS])
                mm.then_inc(cT_done, 1)

            def extra(i, at):
                for stage, c in EXTRA.get((i, at), ()):
                    n = rows_of(c)
                    bank = CHUNK_BANK[c]
                    if stage == "W":
                        pe.wait_ge(ctxT_ready, images_of(c))
                        if c == 0:
                            pe.wait_ge(const_ready, 8)
                        if c in (1, 4):
                            pe.wait_ge(place_ready, {1: 1, 4: 2}[c])
                        for m in range(2):
                            mm = pe.matmul(ps[0:n, bank, 0:D], ctxT[:, m, c * P:c * P + n], wo_sb[:, m, :],
                                           start=(m == 0), stop=(m == 1))
                        mm.then_inc(wo_done, 1)
                    if stage == "X":
                        pe.wait_ge(h2_ready, c + 1)
                        for k in range(KD):
                            mm = pe.transpose(ps[:, bank, D + k * n:D + (k + 1) * n],
                                              h[0:n, c, k * P:(k + 1) * P], ident[0:n, 0:n])
                        mm.then_inc(h2T_done, 1)
                    if stage == "R":
                        pe.wait_ge(h2T_ready, c + 1)
                        for k in range(KD):
                            mm = pe.matmul(ps[0:n, bank, 0:E], xnT[:, k, c * P:c * P + n], wr_c[:, k, :],
                                           start=(k == 0), stop=(k == KD - 1))
                        mm.then_inc(logits_done, 1)
                    if stage == "K":
                        pe.wait_ge(both_ready, c + 1)
                        pe.matmul(ps[0:n, bank, 16:16 + E], ones_bf[0:1, 0:n], base_bf[:, :], start=True, stop=False)
                        for d in range(c):
                            pe.matmul(ps[0:n, bank, 16:16 + E], ones_bf[0:P, 0:n], both[:, d, :],
                                      start=False, stop=False)
                        mm = pe.matmul(ps[0:n, bank, 16:16 + E], upper_bf[0:n, 0:n], both[0:n, c, :],
                                       start=False, stop=True)
                        if c == NC - 1:
                            for d in range(NC):
                                r = rows_of(d)
                                mm = pe.matmul(ps[0:n, bank, 32:32 + E], ones_bf[0:r, 0:n], both[0:r, d, :],
                                               start=(d == 0), stop=(d == NC - 1))
                        mm.then_inc(rank_done, 1)

            project(0)
            first_T(3)
            values(0)
            first_T(4)
            pe.wait_ge(const_ready, 7)
            pe.wait_ge(q_ready, 2)
            pe.wait_ge(k_ready, NKV)
            scores(0, 0)
            scores(0, 1)
            pe.wait_ge(xnT_ready, NC)
            pe.wait_ge(h_ready, NC)
            project(1)
            values(1)
            pe.wait_ge(v_ready, 3)
            for k in range(KD):
                mm = pe.matmul(ps[:, 7, 0:E], mean_of[:, :], wr_sb[:, k, :], start=(k == 0), stop=(k == KD - 1))
            mm.then_inc(colsum_done, 1)
            pe.wait_ge(k_ready, 2 * NKV)
            pe.wait_ge(q_ready, 4)
            scores(1, 0)
            scores(1, 1)
            pe.wait_ge(v_ready, 5)
            probs_T(0)
            for i in range(NG):
                more = i + 2 < NG
                if more:
                    pe.wait_ge(shifted, i + 1)
                    scores(i + 2, 0)
                context(i)
                if i == NG - 2:
                    pe.wait_ge(shifted, NG)
                extra(i, "a")
                if more:
                    scores(i + 2, 1)
                if i + 1 < NG:
                    probs_T(i + 1)
                context_T(i)
                extra(i, "b")

            def rows_T(t, i, k):
                pe.wait_ge(x_in[i], 16 * (k + 1))
                if not (isinstance(t, int) and t == 0):
                    pe.wait_ge(xT_ready, t)
                for m in range(KD):
                    for r in range(2):
                        at = m * CAP + r * CR
                        mm = pe.transpose(ps[:, XT, at:at + CR], x_sb[:, i, r, m * P:(m + 1) * P],
                                          ident[0:CR, 0:CR])
                mm.then_inc(xT_done, 1)

            def width(e):
                return pe.value_load(width_of[0:1, bass.ds(e, 1)], min_val=0, max_val=len(WIDTHS) - 1)

            def by_width(w, product):
                if w is None:
                    product(CR)
                    return

                def up_to(j):
                    if j == 0:
                        product(WIDTHS[0] // 2)
                        return
                    with pe.If(w > j - 1):
                        product(WIDTHS[j] // 2)
                    with pe.Else():
                        up_to(j - 1)

                up_to(len(WIDTHS) - 1)

            def up(t, i, k, w):
                def product(n):
                    pe.wait_ge(wi_in[i], 16 * (k + 1))
                    pe.wait_ge(xT_ready, t + 1)
                    for q in range(FC // 2):
                        if not (isinstance(t, int) and t == 0):
                            pe.wait_ge(hid_ready, FC // 2 * (t - 1) + q + 1)
                        for f in (2 * q, 2 * q + 1):
                            dst = ps[:, UP + q, (f % 2) * CAP:(f % 2 + 1) * CAP].rearrange("p (r n) -> p r n", r=2)
                            for m in range(KD):
                                mm = pe.matmul(dst[:, :, 0:n], wi_sb[:, i, m, f::FC],
                                               x_T[:, m, :].rearrange("p (r n) -> p r n", r=2)[:, :, 0:n],
                                               start=(m == 0), stop=(m == KD - 1))
                        mm.then_inc(up_done, 1)

                by_width(w, product)

            def down(t, i, k, w):
                def product(n):
                    pe.wait_ge(w2_in[i], 16 * (k + 1))
                    for f in range(FC):
                        if f % 2 == 0:
                            pe.wait_ge(hid_ready, FC // 2 * t + f // 2 + 1)
                        for m in range(KD):
                            dst = ps[:, DOWN + m, 0:CAP].rearrange("p (r n) -> p r n", r=2)
                            mm = pe.matmul(dst[:, :, 0:n], w2_sb[:, i, f, m * P:(m + 1) * P],
                                           hidT[:, f, :].rearrange("p (r n) -> p r n", r=2)[:, :, 0:n],
                                           start=(f == 0), stop=(f == FC - 1))
                    mm.then_inc(down_done, 1)

                by_width(w, product)

            def result_T(t):
                pe.wait_ge(yT_ready, t + 1)
                if not (isinstance(t, int) and t == 0):
                    pe.wait_ge(y_ready, t)
                for r in range(2):
                    for k in range(KD):
                        at = r * D + k * P
                        mm = pe.transpose(ps[0:CR, YO, at:at + P], yT[:, k, r * CR:(r + 1) * CR], ident)
                mm.then_inc(yo_done, 1)

            def start(t, i, k, w):
                rows_T(t, i, k)
                up(t, i, k, w)

            def tile(t, i, k, k_next, sized):
                rows_T(t + 1, 1 - i, k_next)
                w = width(t) if sized else None
                down(t, i, k, w)
                w = width(t + 1) if sized else None
                up(t + 1, 1 - i, k_next, w)
                result_T(t)

            def finish(t, i, k, w):
                down(t, i, k, w)
                result_T(t)

            def tiles(first, end, sized):
                tile(first, 0, first // 2, first // 2, sized)
                with pe.Fori(first // 2 + 1, end // 2) as k:
                    tile(2 * k - 1, 1, k - 1, k, sized)
                    tile(2 * k, 0, k, k, sized)

            pe.wait_ge(width_ready, 1)
            start(0, 0, 0, width(0))
            tiles(0, E, True)
            finish(E - 1, 1, E // 2 - 1, width(E - 1))
            with pe.If(over(pe)):
                start(E, 0, E // 2, None)
                tiles(E, T_END, False)
                finish(T_END - 1, 1, T_END // 2 - 1, None)


def kernel(x, L0_tok_W, L0_tok_b, L0_tok_cls_token, L0_tok_pos_embedding, L0_attn_wq, L0_attn_wk, L0_attn_wv,
           L0_attn_wo, L0_ffn_w_router, L0_ffn_wi, L0_ffn_wo):
    import concourse.bacc as bacc
    from concourse.bass_utils import run_bass_kernel_spmd

    x, w, wq, wk, wv, wo = (np.asarray(a) for a in (x, L0_tok_W, L0_attn_wq, L0_attn_wk, L0_attn_wv, L0_attn_wo))
    patches = np.zeros((C * PATCH * PATCH, N), x.dtype)
    patches.reshape(-1, B, S)[:, :, 1:] = \
        x.reshape(B, C, GRID, PATCH, GRID, PATCH).transpose(1, 3, 5, 0, 2, 4).reshape(-1, B, S - 1)

    def by_partition(a):
        return np.ascontiguousarray(a.reshape(a.shape[0] // P, P, -1).transpose(1, 0, 2))

    q = wq.T.reshape(D, NKV, 2, 2, HD).transpose(0, 3, 2, 1, 4).reshape(KD, P, 2, P).transpose(1, 0, 2, 3)
    o = wo.T.reshape(NKV, 2, 2, HD, D).transpose(2, 1, 0, 3, 4).reshape(2, P, D).transpose(1, 0, 2)
    embeddings = np.concatenate([np.asarray(L0_tok_pos_embedding)[0], np.asarray(L0_tok_b)[None],
                                 np.asarray(L0_tok_cls_token)[0]])
    arrays = {
        "patches": by_partition(patches), "w_tok": by_partition(w.T), "embeddings": np.tile(embeddings, (3, 1)),
        "wq": np.ascontiguousarray(q), "wk": by_partition(wk.T), "wv": by_partition(wv.T),
        "wo": np.ascontiguousarray(o), "w_router": np.asarray(L0_ffn_w_router),
        "wi": np.asarray(L0_ffn_wi), "w2": np.asarray(L0_ffn_wo),
        "consts": constants(), "pos_rows": position_rows(),
    }
    nc = bacc.Bacc("TRN2", target_bir_lowering=False, num_devices=1)
    args = [nc.dram_tensor(f"in_{n}", a.shape, mybir.dt.from_np(a.dtype), kind="ExternalInput").ap()
            for n, a in arrays.items()]
    out = nc.dram_tensor("out", (N + CAP, D), F32, kind="ExternalOutput").ap()
    vit_block(nc, *args, out)
    r = run_bass_kernel_spmd(nc, [{f"in_{n}": a for n, a in arrays.items()}], core_ids=[0])
    return r.results[0]["out"][:N].reshape(B, S, D)
```
